# Optimizing a Trainium2 kernel written in Bass

```python
import numpy as np
import jax
import jax.numpy as jnp

def _softmax(x, axis=-1):
    return jax.nn.softmax(x, axis=axis)

def _gelu(x):
    return jax.nn.gelu(x, approximate=True)

def _silu(x):
    return jax.nn.silu(x)

def _sigmoid(x):
    return jax.nn.sigmoid(x)

def _layernorm(x, axis=-1, eps=1e-05):
    m = jnp.mean(x, axis=axis, keepdims=True)
    v = jnp.var(x, axis=axis, keepdims=True)
    return (x - m) / jnp.sqrt(v + eps)

def _scatter_add(tgt, idx, src, axis=0):
    return tgt.at[idx].add(src)

def _segment_sum(src, seg, n):
    return jax.ops.segment_sum(src, seg, n)
kernel_name = 'mk_gnn_preln_d4_gnn_r8_a1e51b'

def setup_inputs(seed: int=0):
    np.random.seed(seed)
    _w = jnp.asarray

    def _rec_inputs():
        import jax
        import jax.numpy as jnp
        _gk = jax.random.key(seed)
        x = -0.0001006 + 1 * jax.random.normal(jax.random.fold_in(_gk, 1), (12500, 96), jnp.float32)
        src = jax.random.randint(jax.random.fold_in(_gk, 2), (200000,), 0, 12500, jnp.int32)
        dst = jax.random.randint(jax.random.fold_in(_gk, 3), (200000,), 0, 12500, jnp.int32)
        _o = jnp.argsort(dst, stable=True)
        src = src[_o]
        dst = dst[_o]
        edge_attr_32 = 0.000196303 + 1.00016 * jax.random.normal(jax.random.fold_in(_gk, 12), (200000, 32), jnp.float32)
        edge_weight = jax.random.uniform(jax.random.fold_in(_gk, 14), (200000,), jnp.float32, 0.0, 1)
        return (x, src, dst, edge_attr_32, edge_weight)
    x, src, dst, edge_attr_32, edge_weight = _rec_inputs()

    def _L0_gnn_setup():
        import jax, jax.numpy as jnp
        import numpy as np
        N_NODES = 6250
        N_EDGES = 100000
        D_FEAT = 96
        D_OUT = 96
        key = jax.random.key(seed)
        ks = jax.random.split(key, 6)
        feat = jax.random.normal(ks[0], (N_NODES, D_FEAT), dtype=jnp.float32)
        affine = jax.random.uniform(ks[1], (N_EDGES,), dtype=jnp.float32)
        mlp_w = jax.random.normal(ks[2], (D_OUT, 2 * D_FEAT), dtype=jnp.float32) * (1.0 / np.sqrt(2 * D_FEAT))
        mlp_b = jax.random.normal(ks[3], (D_OUT,), dtype=jnp.float32) * 0.01
        src_idx = jax.random.randint(ks[4], (N_EDGES,), 0, N_NODES, dtype=jnp.int64)
        dst_idx = jax.random.randint(ks[5], (N_EDGES,), 0, N_NODES, dtype=jnp.int64)
        return {'feat': feat, 'affine': affine, 'mlp_w': mlp_w, 'mlp_b': mlp_b, 'src_idx': src_idx, 'dst_idx': dst_idx}
    _L0_gnn_all = _L0_gnn_setup()
    _L0_gnn_in = {k: v for k, v in _L0_gnn_all.items() if k in ('mlp_w', 'mlp_b')}
    del _L0_gnn_all

    def _L1_gnn_setup():
        import jax, jax.numpy as jnp
        import numpy as np
        N_NODES = 6250
        N_EDGES = 100000
        IN_DIM = 96
        OUT_DIM = 96
        EDGE_DIM = 32
        BN_EPS = 1e-05
        key = jax.random.key(seed)
        ks = jax.random.split(key, 12)
        x = jax.random.normal(ks[0], (N_NODES, IN_DIM), dtype=jnp.float32)
        edge_index = jax.random.randint(ks[1], (2, N_EDGES), 0, N_NODES, dtype=jnp.int64)
        edge_attr = jax.random.normal(ks[2], (N_EDGES, EDGE_DIM), dtype=jnp.float32)
        We = jax.random.normal(ks[3], (EDGE_DIM, IN_DIM), dtype=jnp.float32) / np.sqrt(EDGE_DIM)
        be = jnp.zeros((IN_DIM,), dtype=jnp.float32)
        W1 = jax.random.normal(ks[4], (IN_DIM, OUT_DIM), dtype=jnp.float32) / np.sqrt(IN_DIM)
        b1 = jnp.zeros((OUT_DIM,), dtype=jnp.float32)
        W2 = jax.random.normal(ks[5], (OUT_DIM, OUT_DIM), dtype=jnp.float32) / np.sqrt(OUT_DIM)
        b2 = jnp.zeros((OUT_DIM,), dtype=jnp.float32)
        gamma = jnp.ones((OUT_DIM,), dtype=jnp.float32)
        beta = jnp.zeros((OUT_DIM,), dtype=jnp.float32)
        return {'x': x, 'edge_index': edge_index, 'edge_attr': edge_attr, 'We': We, 'be': be, 'W1': W1, 'b1': b1, 'W2': W2, 'b2': b2, 'gamma': gamma, 'beta': beta}
    _L1_gnn_all = _L1_gnn_setup()
    _L1_gnn_in = {k: v for k, v in _L1_gnn_all.items() if k in ('We', 'be', 'W1', 'b1', 'W2', 'b2', 'gamma', 'beta')}
    del _L1_gnn_all

    def _L2_gnn_setup():
        import jax, jax.numpy as jnp
        import numpy as np
        EPS = 1e-07
        BETA = 1.0
        key = jax.random.key(seed)
        k1, k2, k3, k4 = jax.random.split(key, 4)
        N, E, D_IN, D_OUT = (6250, 100000, 96, 96)
        feat = jax.random.normal(k1, (N, D_IN), dtype=jnp.float32)
        src = jax.random.randint(k2, (E,), 0, N, dtype=jnp.int32)
        dst = jax.random.randint(k3, (E,), 0, N, dtype=jnp.int32)
        W = jax.random.normal(k4, (D_IN, D_OUT), dtype=jnp.float32) / np.sqrt(D_IN)
        b = jnp.zeros((D_OUT,), dtype=jnp.float32)
        return {'feat': feat, 'src': src, 'dst': dst, 'W': W, 'b': b}
    _L2_gnn_all = _L2_gnn_setup()
    _L2_gnn_in = {k: v for k, v in _L2_gnn_all.items() if k in ('W', 'b')}
    del _L2_gnn_all

    def _L3_gnn_setup():
        import jax, jax.numpy as jnp
        import numpy as np
        N_NODES = 6250
        N_EDGES = 100000
        D_IN = 96
        D_OUT = 96
        NEG_SLOPE = 0.2
        key = jax.random.key(seed)
        k1, k2, k3, k4, k5 = jax.random.split(key, 5)
        x = jax.random.normal(k1, (N_NODES, D_IN), dtype=jnp.float32)
        W = jax.random.normal(k2, (D_IN, D_OUT), dtype=jnp.float32) * (1.0 / np.sqrt(D_IN))
        att_src = jax.random.normal(k3, (D_OUT,), dtype=jnp.float32) * 0.1
        att_dst = jax.random.normal(k4, (D_OUT,), dtype=jnp.float32) * 0.1
        bias = jnp.zeros((D_OUT,), dtype=jnp.float32)
        edge_index = jax.random.randint(k5, (2, N_EDGES), 0, N_NODES, dtype=jnp.int64)
        return {'x': x, 'W': W, 'att_src': att_src, 'att_dst': att_dst, 'bias': bias, 'edge_index': edge_index}
    _L3_gnn_all = _L3_gnn_setup()
    _L3_gnn_in = {k: v for k, v in _L3_gnn_all.items() if k in ('W', 'att_src', 'att_dst', 'bias')}
    del _L3_gnn_all
    return {'x': x, 'src': src, 'dst': dst, 'edge_attr_32': edge_attr_32, 'edge_weight': edge_weight, 'L0_gnn_mlp_w': _L0_gnn_in['mlp_w'], 'L0_gnn_mlp_b': _L0_gnn_in['mlp_b'], 'L1_gnn_We': _L1_gnn_in['We'], 'L1_gnn_be': _L1_gnn_in['be'], 'L1_gnn_W1': _L1_gnn_in['W1'], 'L1_gnn_b1': _L1_gnn_in['b1'], 'L1_gnn_W2': _L1_gnn_in['W2'], 'L1_gnn_b2': _L1_gnn_in['b2'], 'L1_gnn_gamma': _L1_gnn_in['gamma'], 'L1_gnn_beta': _L1_gnn_in['beta'], 'L2_gnn_W': _L2_gnn_in['W'], 'L2_gnn_b': _L2_gnn_in['b'], 'L3_gnn_W': _L3_gnn_in['W'], 'L3_gnn_att_src': _L3_gnn_in['att_src'], 'L3_gnn_att_dst': _L3_gnn_in['att_dst'], 'L3_gnn_bias': _L3_gnn_in['bias']}

def reference(x, src, dst, edge_attr_32, edge_weight, L0_gnn_mlp_w, L0_gnn_mlp_b, L1_gnn_We, L1_gnn_be, L1_gnn_W1, L1_gnn_b1, L1_gnn_W2, L1_gnn_b2, L1_gnn_gamma, L1_gnn_beta, L2_gnn_W, L2_gnn_b, L3_gnn_W, L3_gnn_att_src, L3_gnn_att_dst, L3_gnn_bias):
    import jax
    import jax.numpy as jnp

    def _L0_gnn_ref(feat, affine, mlp_w, mlp_b, src_idx, dst_idx):
        import jax, jax.numpy as jnp
        import numpy as np
        N_NODES = 6250
        N_EDGES = 100000
        D_FEAT = 96
        D_OUT = 96
        msgs = feat[src_idx] * affine[:, None]
        agg = jax.ops.segment_sum(msgs, dst_idx, num_segments=feat.shape[0])
        gcn_feat = jnp.concatenate([feat, agg], axis=-1)
        out = gcn_feat @ mlp_w.T + mlp_b
        return out

    def _L1_gnn_ref(x, edge_index, edge_attr, We, be, W1, b1, W2, b2, gamma, beta):
        import jax, jax.numpy as jnp
        import numpy as np
        N_NODES = 6250
        N_EDGES = 100000
        IN_DIM = 96
        OUT_DIM = 96
        EDGE_DIM = 32
        BN_EPS = 1e-05
        src = edge_index[0]
        dst = edge_index[1]
        msg = jax.nn.relu(x[src] + edge_attr @ We + be)
        aggr = jax.ops.segment_sum(msg, dst, num_segments=x.shape[0])
        h = x + aggr
        h = jax.nn.relu(h @ W1 + b1) @ W2 + b2
        mean = jnp.mean(h, axis=0)
        var = jnp.mean(jnp.square(h - mean), axis=0)
        h = (h - mean) * jax.lax.rsqrt(var + BN_EPS) * gamma + beta
        return jax.nn.relu(h)

    def _L2_gnn_ref(feat, src, dst, W, b):
        import jax, jax.numpy as jnp
        import numpy as np
        EPS = 1e-07
        BETA = 1.0
        N = feat.shape[0]
        m = jax.nn.relu(feat[src]) + EPS
        logits = BETA * m
        seg_max = jax.ops.segment_max(logits, dst, num_segments=N)
        ex = jnp.exp(logits - seg_max[dst])
        denom = jax.ops.segment_sum(ex, dst, num_segments=N)
        a = ex / denom[dst]
        msg = jax.ops.segment_sum(a * m, dst, num_segments=N)
        feats = feat + msg
        return feats @ W + b

    def _L3_gnn_ref(x, W, att_src, att_dst, bias, edge_index):
        import jax, jax.numpy as jnp
        import numpy as np
        N_NODES = 6250
        N_EDGES = 100000
        D_IN = 96
        D_OUT = 96
        NEG_SLOPE = 0.2
        N = x.shape[0]
        h = x @ W
        loops = jnp.arange(N, dtype=edge_index.dtype)
        src = jnp.concatenate([edge_index[0], loops])
        dst = jnp.concatenate([edge_index[1], loops])
        a_src = h @ att_src
        a_dst = h @ att_dst
        e = jax.nn.leaky_relu(a_src[src] + a_dst[dst], NEG_SLOPE)
        m = jax.ops.segment_max(e, dst, num_segments=N)
        e = jnp.exp(e - m[dst])
        denom = jax.ops.segment_sum(e, dst, num_segments=N)
        alpha = e / (denom[dst] + 1e-16)
        out = jax.ops.segment_sum(h[src] * alpha[:, None], dst, num_segments=N)
        return jnp.tanh(out + bias)
    edge_index = jnp.stack([src, dst])
    h = jnp.maximum(_layernorm(x, axis=-1), 0.0)
    x = x + _L0_gnn_ref(h, edge_weight, L0_gnn_mlp_w, L0_gnn_mlp_b, src, dst)
    h = jnp.maximum(_layernorm(x, axis=-1), 0.0)
    x = x + _L1_gnn_ref(h, edge_index, edge_attr_32, L1_gnn_We, L1_gnn_be, L1_gnn_W1, L1_gnn_b1, L1_gnn_W2, L1_gnn_b2, L1_gnn_gamma, L1_gnn_beta)
    h = jnp.maximum(_layernorm(x, axis=-1), 0.0)
    x = x + _L2_gnn_ref(h, src, dst, L2_gnn_W, L2_gnn_b)
    h = jnp.maximum(_layernorm(x, axis=-1), 0.0)
    x = x + _L3_gnn_ref(h, L3_gnn_W, L3_gnn_att_src, L3_gnn_att_dst, L3_gnn_bias, edge_index)
    return x

_drawn_inputs = setup_inputs


def setup_inputs(seed=0):
    import zlib

    import numpy as np

    out = dict(_drawn_inputs(seed))
    spreads = {'L1_gnn_be': (0.0, 0.267),
     'L1_gnn_b1': (0.0, 2.0),
     'L1_gnn_b2': (0.0, 2.0),
     'L1_gnn_gamma': (1.0, 0.2),
     'L1_gnn_beta': (0.0, 0.29),
     'L2_gnn_b': (0.0, 0.1),
     'L3_gnn_bias': (0.0, 0.321)}
    factors = {'L0_gnn_mlp_b': 8.0, 'L3_gnn_att_src': 8.0, 'L3_gnn_att_dst': 29.934}
    for name, (base, spread) in spreads.items():
        noise = np.random.default_rng([zlib.crc32(name.encode()), seed]).standard_normal(out[name].shape)
        drawn = base * np.exp(spread * noise) if base else spread * noise
        out[name] = jnp.asarray(drawn.astype(out[name].dtype))
    for name, factor in factors.items():
        out[name] = (out[name] * factor).astype(out[name].dtype)
    return out
```

```python
from contextlib import ExitStack

import numpy as np

import concourse.bass as bass
from concourse import mybir

F32 = mybir.dt.float32
BF16 = mybir.dt.bfloat16
I32 = mybir.dt.int32
ALU = mybir.AluOpType
ACT = mybir.ActivationFunctionType
AX = mybir.AxisListType.X
P = 128
D = 96
DE = 32
RING = 16
HALF = RING // 2
NO_NODE = 1 << 20
BIG = 1e30
LN_EPS = 1e-5
BN_EPS = 1e-5
SOFT_EPS = 1e-7
GAT_EPS = 1e-16
SLOPE = 0.2


class Sizes:
    def __init__(self, nodes, edges):
        self.N, self.E = nodes, edges
        self.NB = -(-nodes // P)
        self.NB += self.NB % 2
        self.LAST = nodes - (self.NB - 1) * P
        self.TILES = -(-edges // P)
        self.ITERS = -(-(self.TILES + self.NB - 1) // RING)
        self.STEPS = self.ITERS * RING
        self.SCH = -(-self.STEPS // P)
        self.SW = self.SCH * P
        rows = max(self.TILES, self.SW - self.NB + 1)
        self.TR = rows + (-rows) % 4
        self.DU = max(u for u in range(2, 17, 2) if self.NB % u == 0)
        assert self.LAST > 0 and D * self.NB >= RING * P + self.SW and 2 * D * self.NB >= self.TR + 7 * self.SW and self.STEPS % 4 == 0 and self.STEPS // 4 <= 512 and self.TR // 4 <= 512


def build(nc, z, x, src, dst, ew, eaT, w0T, b0, We, be, W1, b1, W2, b2, gamma, beta, W3, b3, W4, W4T, att, bias4, out):
    NB, SCH, SW, STEPS, ITERS, TR, DU = z.NB, z.SCH, z.SW, z.STEPS, z.ITERS, z.TR, z.DU
    ctx = ExitStack()
    with ctx:
        def sb(name, shape, dt=F32):
            return ctx.enter_context(nc.sbuf_tensor(name, shape, dt))

        def sem(name):
            return ctx.enter_context(nc.semaphore(name))

        tab = [nc.dram_tensor(f"table{i}", (NB * P, w), F32).ap() for i, w in enumerate((D, D, 2 * D, D + 2))]
        ad_dram = nc.dram_tensor("ad_dram", (NB, P), F32).ap()

        X = sb("X", [P, NB, D])
        R = sb("R", [P, NB * 3 * D])
        H = R[:, 2 * D * NB:3 * D * NB].rearrange("p (b f) -> p b f", f=D)
        A = R[:, 0:D * NB].rearrange("p (b f) -> p b f", f=D)
        A2 = R[:, 0:2 * D * NB].rearrange("p (b f) -> p b f", f=2 * D)
        A3 = R[:, 0:(D + 2) * NB].rearrange("p (b f) -> p b f", f=D + 2)
        adrow = R[:, (D + 2) * NB:(D + 2 + P) * NB]
        cmp = R[:, 0:TR]
        reach = R[:, TR:TR + SW]
        srow = R[:, TR + 4 * SW:TR + 5 * SW]
        bcast_src = R[:, TR + 5 * SW:TR + 5 * SW + max(TR, SW)]
        erow = [R[:, TR + SW + i * SW:TR + SW + (i + 1) * SW].rearrange("p (c e) -> p c e", e=P) for i in range(3)]
        ering = sb("gathered_rows", [P, RING, 2 * D])
        work = sb("work", [P, 8 * D + 12 * P])
        raw, msg, pre, sel = (work[:, i * 4 * P:(i + 1) * 4 * P].rearrange("p (r e) -> p r e", r=4) for i in range(4))
        stg = work[:, 0:8 * D].rearrange("p (r f) -> p r f", r=4)
        tT = work[0:D, 8 * D:8 * D + 8 * P].rearrange("p (r n) -> p r n", r=4)
        rT = work[0:D, 8 * D + 8 * P:8 * D + 12 * P].rearrange("p (r n) -> p r n", r=4)
        zb = sb("off_block", [P, 4, P], BF16)
        eatt = R[0:DE + 1, D * NB:D * NB + RING * P].rearrange("p (k e) -> p k e", k=RING)
        ib = sb("staged_index", [P, RING], I32)
        idx = sb("src_of_step", [P, SW], I32)
        dstl = sb("dst_in_block", [P, SW])
        wst = sb("weight_of_step", [P, SW])
        brow = sb("block_of_step", [1, SW], I32)
        trow = R[0:1, 2 * D * NB - SW:2 * D * NB].bitcast(I32)
        iota = sb("iota", [P, P])
        iobf = sb("iota_bf", [P, P], BF16)
        ident = sb("ident", [P, P])
        idbf = sb("ident_bf", [P, P], BF16)
        nidbf = sb("neg_ident_bf", [P, P], BF16)
        ones = sb("ones", [P, P])
        col = sb("cols", [P, 16])
        scol = sb("step_col", [P, SCH])
        bcol = sb("block_col", [P, SCH])
        tcol = sb("tile_col", [P, SCH])
        ti = sb("tile_idx", [P, SCH], I32)
        st1 = sb("ln_mean", [P, NB])
        st2 = sb("ln_rstd", [P, NB])
        w0 = sb("w0", [D, 2, D])
        wew = sb("we", [DE + 1, D])
        w1 = sb("w1", [D, D])
        w2 = sb("w2", [D, D])
        w3 = sb("w3", [D, D])
        w4x = sb("w4x", [D, D + 3])
        w4t = sb("w4t", [D, D])
        att2 = sb("att2", [D, 2])
        b1c = sb("b1c", [D, 1])
        brows = sb("bias_rows", [1, 3, D])
        bn = sb("bn_rows", [P, 3, D])
        bs = sb("bn_stats", [P, 3, D])
        adc = sb("ad_col", [P, NB])
        adT = sb("ad_T", [NB, P])
        lc = sb("run_max", [P, NB])
        cm = sb("tile_max", [P, RING])
        ln_ = sb("new_max", [P, RING])
        df = sb("max_drop", [P, RING])
        fac = sb("rescale", [P, RING])
        PS = ctx.enter_context(nc.psum_tensor("PS", [P, 8, 512], F32))

        s_in = sem("inputs_loaded")
        s_w = sem("weights_loaded")
        s_io = sem("pool_consts")
        s_dp = sem("dve_prep")
        s_pp = sem("pe_prep")
        s_er = sem("edge_rows_gathered")
        s_dch = sem("dve_chain")
        s_ach = sem("act_chain")
        s_v2a = sem("dve_to_act")
        s_a2v = sem("act_to_dve")
        s_bnp = sem("bn_summed")
        tab_ready = [sem(f"table_values{i}") for i in range(4)]
        tab_wr = [sem(f"table_written{i}") for i in range(4)]
        staged = [sem(f"index_staged{h}") for h in range(2)]
        gat = [sem(f"gathered{k}") for k in range(RING)]
        eah = [sem(f"edge_features_loaded{h}") for h in range(2)]
        slot_free = sem("slot_free")
        sel_rdy = sem("one_hot_ready")
        added = sem("block_added")
        ea_mm = sem("edge_product_ready")
        pre_rdy = sem("pre_message_ready")
        msg_rdy = sem("message_ready")
        raw_rdy = sem("raw_logits_ready")
        u_rdy = sem("logits_ready")
        z_rdy = sem("off_block_ready")
        psa = sem("logits_turned")
        cmx = sem("tile_max_ready")
        lcn = sem("new_max_ready")
        dfr = sem("max_drop_ready")
        lcs = sem("run_max_stored")
        psc = sem("max_rows_ready")
        xrd = sem("shifted_ready")
        prd = sem("weights_ready")
        frd = sem("rescale_ready")
        d_st = sem("dense_staged")
        d_tr = sem("dense_turned")
        d_tc = sem("dense_turned_copied")
        d_m1 = sem("dense_product1")
        d_re = sem("dense_relu")
        d_m2 = sem("dense_product2")
        d_po = sem("dense_done")
        s_adT = sem("ad_turned")
        s_adS = sem("ad_copied")
        s_adD = sem("ad_in_dram")
        s_adR = sem("ad_rows_loaded")
        s_fin = sem("result_ready")
        s_out = sem("result_stored")

        block = ctx.enter_context(nc.Block())

        def gat_val(L, g):
            return g * 16 + (16 * (L * ITERS) + 16)

        def lagged(n, *stages):
            top = max(l for l, _ in stages)
            for i in range(n + top):
                for lag, fn in stages:
                    if 0 <= i - lag < n:
                        fn(i - lag)

        @block.sync
        def _(sp):
            with nc.allow_non_contiguous_dma(reason="one destination per tile"):
                sp.dma_start(cmp[0:1, 0:TR].bitcast(I32), dst[:, P - 1:P].rearrange("t a -> a t")).then_inc(s_in, 16)
            sp.wait_ge(s_io, 1)
            sp.dma_start(X[:, 0:NB - 1, :], x[0:(NB - 1) * P, :].rearrange("(b p) f -> p b f", p=P)).then_inc(s_w, 16)
            sp.dma_start(X[0:z.LAST, NB - 1, :], x[(NB - 1) * P:z.N, :]).then_inc(s_w, 16)
            sp.dma_start(w0[:, :, :], w0T.rearrange("(h i) o -> i h o", h=2)).then_inc(s_w, 16)
            sp.dma_start(wew[0:DE, :], We).then_inc(s_w, 16)
            sp.dma_start(wew[DE:DE + 1, :], be.rearrange("(a n) -> a n", a=1)).then_inc(s_w, 16)
            for t, s in ((w1, W1), (w2, W2), (w3, W3), (w4t, W4T)):
                sp.dma_start(t[:, :], s).then_inc(s_w, 16)
            sp.dma_start(w4x[:, 0:D], W4).then_inc(s_w, 16)
            sp.dma_start(att2[:, :], att).then_inc(s_w, 16)
            sp.dma_start(b1c[:, :], b1.rearrange("(n a) -> n a", a=1)).then_inc(s_w, 16)
            for i, s in enumerate((b0, b2, b3)):
                sp.dma_start(brows[:, i, :], s.rearrange("(a n) -> a n", a=1)).then_inc(s_w, 16)
            for i, s in enumerate((gamma, beta, bias4)):
                sp.dma_start(bn[:, i, :], s.rearrange("(a n) -> a n", a=1).broadcast_to([P, D])).then_inc(s_w, 16)

            for L in range(4):
                sp.wait_ge(tab_ready[L], 1)
                vals = (H, H, A2, A3)[L]
                sp.dma_start(tab[L].rearrange("(b p) f -> p b f", p=P), vals).then_inc(tab_wr[L], 16)
                if L == 3:
                    sp.wait_ge(s_adS, 1)
                    sp.dma_start(ad_dram, adT[:, :]).then_inc(s_adD, 16)
                    sp.wait_ge(s_adD, 16)
                    sp.dma_start(adrow, ad_dram.rearrange("(a b) p -> a (b p)", a=1).broadcast_to([P, NB * P]))\
                        .then_inc(s_adR, 16)
                with sp.Fori(0, ITERS) as g:
                    for h in range(2):
                        sp.wait_ge(slot_free, g * RING + (L * STEPS + HALF * h + HALF))
                        sp.dma_start(ib[:, h * HALF:(h + 1) * HALF], idx[:, bass.DynSlice(g * RING + h * HALF, HALF)])\
                            .then_inc(staged[h], 16)
                        if L == 1:
                            for k in range(h * HALF, (h + 1) * HALF):
                                t = sp.value_load(trow[0:1, bass.DynSlice(g * RING + k, 1)], min_val=0, max_val=TR - 1)
                                sp.dma_start(eatt[0:DE, k, :], eaT[bass.DynSlice(t, 1), :, :].rearrange("a f e -> (a f) e"))\
                                    .then_inc(eah[h], 16)
            sp.wait_ge(s_fin, 1)
            sp.dma_start(out[0:(NB - 1) * P, :].rearrange("(b p) f -> p b f", p=P), X[:, 0:NB - 1, :]).then_inc(s_out, 16)
            sp.dma_start(out[(NB - 1) * P:z.N, :], X[0:z.LAST, NB - 1, :]).then_inc(s_out, 16)
            sp.wait_ge(s_out, 32)

        @block.gpsimd
        def _(pool):
            pool.memset(X[:, NB - 1, :], 0.0).then_inc(s_io, 1)
            pool.iota(iota[:, :], pattern=[[1, P]], base=0, channel_multiplier=0, allow_small_or_imprecise_dtypes=True).then_inc(s_io, 1)
            pool.iota(iobf[:, :], pattern=[[1, P]], base=0, channel_multiplier=0, allow_small_or_imprecise_dtypes=True).then_inc(s_io, 1)
            pool.iota(reach, pattern=[[1, SW]], base=0, channel_multiplier=0, allow_small_or_imprecise_dtypes=True).then_inc(s_io, 1)
            pool.iota(srow[0:1, :], pattern=[[1, SW]], base=0, channel_multiplier=0, allow_small_or_imprecise_dtypes=True).then_inc(s_io, 1)
            pool.iota(scol[:, :], pattern=[[P, SCH]], base=0, channel_multiplier=1, allow_small_or_imprecise_dtypes=True).then_inc(s_io, 1)
            pool.iota(col[:, 0:1], pattern=[[0, 1]], base=0, channel_multiplier=1, allow_small_or_imprecise_dtypes=True).then_inc(s_io, 1)
            pool.iota(col[:, 1:2], pattern=[[0, 1]], base=P, channel_multiplier=P, allow_small_or_imprecise_dtypes=True).then_inc(s_io, 1)
            pool.memset(ones[:, :], 1.0).then_inc(s_io, 1)
            pool.memset(ident[:, :], 0.0).then_inc(s_io, 1)
            pool.memset(idbf[:, :], 0.0).then_inc(s_io, 1)
            pool.memset(nidbf[:, :], 0.0).then_inc(s_io, 1)
            pool.wait_ge(s_io, 12)
            for m, v in ((ident, 1.0), (idbf, 1.0), (nidbf, -1.0)):
                pool.affine_select(out=m[:, :], in_=m[:, :], compare_op=ALU.not_equal, fill=v, base=0,
                                   pattern=[[-1, P]], channel_multiplier=1).then_inc(s_io, 1)
            pool.wait_ge(s_dp, 3)
            for c in range(SCH):
                for r, t in zip(erow, (src, dst, ew)):
                    o = r[:, c, :] if t is ew else r[:, c, :].bitcast(I32)
                    pool.indirect_dma_start(o, None, t, bass.IndirectOffsetOnAxis(ap=ti[:, c:c + 1], axis=0))\
                        .then_inc(s_er, 16)
            for L in range(4):
                pool.wait_ge(tab_wr[L], 16)
                W = (D, D, 2 * D, D + 2)[L]
                with pool.Fori(0, ITERS) as g:
                    for h in range(2):
                        pool.wait_ge(staged[h], g * 16 + (16 * (L * ITERS) + 16))
                        pool.nop(nofuse=True)
                        for k in range(h * HALF, (h + 1) * HALF):
                            pool.indirect_dma_start(ering[:, k, 0:W], None, tab[L],
                                                    bass.IndirectOffsetOnAxis(ap=ib[:, k:k + 1], axis=0)).then_inc(gat[k], 16)

        @block.tensor
        def _(pe):
            pe.sem_inc(slot_free, RING)
            pe.sem_inc(d_tr, 4)
            pe.wait_ge(s_io, 15)
            pe.wait_ge(s_dp, 1)
            q = TR // 4
            for i in range(4):
                last = pe.matmul(PS[:, i, 0:q], ones[0:1, :], bcast_src[0:1, i * q:(i + 1) * q], start=True, stop=True)
            last.then_inc(s_pp, 1)
            pe.wait_ge(s_dp, 2)
            for c in range(SCH):
                pe.matmul(PS[:, 4, c:c + 1], reach[0:NB - 1, c * P:(c + 1) * P], ones[0:NB - 1, 0:1], start=True, stop=True)
            q = SW // 4
            for i in range(4):
                last = pe.matmul(PS[0:1, (5, 6, 7, 0)[i], 0:q], ones[0:NB - 1, 0:1], reach[0:NB - 1, i * q:(i + 1) * q],
                                 start=True, stop=True)
            last.then_inc(s_pp, 1)
            pe.wait_ge(s_dp, 4)
            for i in range(3 * SCH):
                if i >= 8:
                    pe.wait_ge(s_dp, 4 + i - 7)
                pe.transpose(PS[:, i % 8, 0:P], erow[i % 3][:, i // 3, :], ident[:, :]).then_inc(s_pp, 1)
            pe.wait_ge(s_w, 16 * 18)
            pe.wait_ge(s_dp, 4 + 3 * SCH)
            pe.matmul(PS[0:D, 0, 0:2], w4t[:, :], att2[:, :], start=True, stop=True).then_inc(s_pp, 1)
            base_pp = 2 + 3 * SCH + 1

            def dense(d):
                halves = 2 if d == 0 else 1

                def turn(g, i):
                    pe.wait_ge(d_st, g * DU + (d * NB + i + 1))
                    for q in range(halves):
                        last = pe.transpose(PS[0:D, i % 2, q * P:(q + 1) * P], stg[:, i % 4, q * D:(q + 1) * D], ident[:, :])
                    last.then_inc(d_tr, 1)

                def product1(g, i):
                    pe.wait_ge(d_tc, g * DU + (d * NB + i + 1))
                    o = PS[:, 2 + i % 2, 0:(D + 3 if d == 3 else D)]
                    t = tT[:, i % 4, :]
                    if d == 0:
                        pe.matmul(o, t[:, 0:P], w0[:, 0, :], start=True, stop=False)
                        pe.matmul(o, t[:, P:2 * P], w0[:, 1, :], start=False, stop=False)
                        pe.matmul(o, ones[0:1, :], brows[:, 0, :], start=False, stop=True).then_inc(d_m1, 1)
                    elif d == 1:
                        pe.matmul(PS[0:D, 2 + i % 2, 0:P], w1[:, :], t[:, 0:P], start=True, stop=True).then_inc(d_m1, 1)
                    elif d == 2:
                        pe.matmul(o, t[:, 0:P], w3[:, :], start=True, stop=False)
                        pe.matmul(o, ones[0:1, :], brows[:, 2, :], start=False, stop=True).then_inc(d_m1, 1)
                    else:
                        pe.matmul(o, t[:, 0:P], w4x[:, :], start=True, stop=True).then_inc(d_m1, 1)

                def product2(g, i):
                    pe.wait_ge(d_re, g * DU + (i + 1))
                    o = PS[:, 4 + i % 4, 0:D]
                    pe.matmul(o, rT[:, i % 4, :], w2[:, :], start=True, stop=False)
                    pe.matmul(o, ones[0:1, :], brows[:, 1, :], start=False, stop=True).then_inc(d_m2, 1)

                with pe.Fori(0, NB // DU) as g:
                    stages = [(0, lambda i: turn(g, i)), (1, lambda i: product1(g, i))]
                    if d == 1:
                        stages.append((2, lambda i: product2(g, i)))
                    lagged(DU, *stages)

            def steps(L):
                base = L * STEPS
                W = (D, D, 2 * D)[L]

                def edge_product(g, k):
                    pe.wait_ge(eah[k // HALF], g * (16 * HALF) + 16 * HALF)
                    pe.matmul(PS[:, 4 + k % 4, 0:D], eatt[:, k, :], wew[:, :], start=True, stop=True).then_inc(ea_mm, 1)

                def sum_tile(g, k):
                    pe.wait_ge(sel_rdy, g * RING + (base + k + 1))
                    if L == 1:
                        pe.wait_ge(msg_rdy, g * RING + (k + 1))
                        rhs = msg[:, k % 4, 0:D]
                    else:
                        pe.wait_ge(gat[k], gat_val(L, g))
                        rhs = ering[:, k, 0:W]
                    pe.matmul(PS[:, k % 4, 0:W], sel[:, k % 4, :], rhs, start=True, stop=True).then_inc(slot_free, 1)

                with pe.Fori(0, ITERS) as g:
                    if L == 1:
                        lagged(RING, (0, lambda k: edge_product(g, k)), (2, lambda k: sum_tile(g, k)))
                    else:
                        lagged(RING, (0, lambda k: sum_tile(g, k)))

            def attention_steps():
                def turn_logits(g, k):
                    pe.wait_ge(u_rdy, g * RING + (k + 1))
                    pe.wait_ge(z_rdy, g * RING + (k + 1))
                    o = PS[:, k % 2, 0:P]
                    pe.matmul(o, msg[:, k % 4, :], ident[:, :], start=True, stop=False)
                    pe.matmul(o, zb[:, k % 4, :], idbf[:, :], start=False, stop=True).then_inc(psa, 1)

                def spread_max(g, k):
                    pe.wait_ge(lcn, g * RING + (k + 1))
                    o = PS[:, 2 + k % 2, 0:P]
                    pe.matmul(o, ln_[:, k:k + 1].broadcast_to([P, P]), ident[:, :], start=True, stop=False)
                    pe.matmul(o, nidbf[:, :], zb[:, k % 4, :], start=False, stop=True).then_inc(psc, 1)

                def sum_tile(g, k):
                    pe.wait_ge(prd, g * RING + (k + 1))
                    pe.wait_ge(gat[k], gat_val(3, g))
                    pe.matmul(PS[:, 4 + k % 2, 0:D + 1], sel[:, k % 4, :], ering[:, k, 0:D + 1], start=True, stop=True)\
                        .then_inc(slot_free, 1)

                with pe.Fori(0, ITERS) as g:
                    lagged(RING, (0, lambda k: turn_logits(g, k)), (1, lambda k: spread_max(g, k)),
                           (3, lambda k: sum_tile(g, k)))

            steps(0)
            dense(0)
            steps(1)
            dense(1)
            for i in range(2):
                pe.wait_ge(s_bnp, 2 * i + 1)
                pe.matmul(PS[:, i, 0:D], ones[:, :], bs[:, i, :], start=True, stop=True).then_inc(s_bnp, 1)
            steps(2)
            dense(2)
            dense(3)
            pe.wait_ge(d_po, 4 * NB)
            pe.transpose(PS[0:NB, 6, 0:P], adc[:, :], ident[:, :]).then_inc(s_adT, 1)
            attention_steps()

        @block.scalar
        def _(act):
            n = [0]

            def link(ins):
                n[0] += 1
                ins.then_inc(s_ach, 1)
                act.wait_ge(s_ach, n[0])

            def norm(i):
                act.wait_ge(s_v2a, 3 * i + 1)
                act.activation(A, H, ACT.Square).then_inc(s_a2v, 1)
                act.wait_ge(s_v2a, 3 * i + 2)
                act.activation(st2[:, :], st2[:, :], ACT.Sqrt).then_inc(s_a2v, 1)
                act.wait_ge(s_v2a, 3 * i + 3)
                ins = act.activation(H, H, ACT.Relu)
                ins.then_inc(s_a2v, 1)

            def dense(d):
                def stage(g, i):
                    act.wait_ge(d_tr, g * DU + (d * NB + max(i + 1, 4)))
                    b = g * DU + i
                    if d == 0:
                        act.copy(stg[:, i % 4, 0:D], H[:, bass.DynSlice(b, 1), :].rearrange("p a f -> p (a f)"))
                        act.copy(stg[:, i % 4, D:2 * D], A[:, bass.DynSlice(b, 1), :].rearrange("p a f -> p (a f)")).then_inc(d_st, 1)
                    else:
                        act.copy(stg[:, i % 4, 0:D], H[:, bass.DynSlice(b, 1), :].rearrange("p a f -> p (a f)")).then_inc(d_st, 1)

                def relu(g, i):
                    act.wait_ge(d_m1, g * DU + (d * NB + i + 1))
                    act.activation(rT[:, i % 4, :], PS[0:D, 2 + i % 2, 0:P], ACT.Relu, bias=b1c[:, 0:1]).then_inc(d_re, 1)

                with act.Fori(0, NB // DU) as g:
                    if d == 1:
                        lagged(DU, (0, lambda i: stage(g, i)), (1, lambda i: relu(g, i)))
                    else:
                        lagged(DU, (0, lambda i: stage(g, i)))

            norm(0)
            act.wait_ge(added, 1 + STEPS)
            dense(0)
            norm(1)
            with act.Fori(0, ITERS) as g:
                for k in range(RING):
                    act.wait_ge(pre_rdy, g * RING + (k + 1))
                    act.activation(msg[:, k % 4, 0:D], pre[:, k % 4, 0:D], ACT.Relu).then_inc(msg_rdy, 1)
            act.wait_ge(s_v2a, 7)
            dense(1)
            act.wait_ge(s_v2a, 8)
            act.activation(A, H, ACT.Square).then_inc(s_a2v, 1)
            act.wait_ge(s_v2a, 9)
            act.activation(bs[:, 1, :], bs[:, 1, :], ACT.Sqrt).then_inc(s_a2v, 1)
            act.wait_ge(s_v2a, 10)
            act.activation(H, H, ACT.Relu).then_inc(s_a2v, 1)
            act.wait_ge(s_v2a, 11)
            act.activation(A, H, ACT.Square).then_inc(s_a2v, 1)
            act.wait_ge(s_v2a, 12)
            act.activation(st2[:, :], st2[:, :], ACT.Sqrt).then_inc(s_a2v, 1)
            act.wait_ge(s_v2a, 13)
            link(act.activation(H, H, ACT.Relu))
            act.activation(A2[:, :, 0:D], H, ACT.Exp, bias=col[:, 3:4]).then_inc(s_a2v, 1)
            act.wait_ge(s_v2a, 14)
            dense(2)
            act.wait_ge(s_v2a, 15)
            act.activation(A, H, ACT.Square).then_inc(s_a2v, 1)
            act.wait_ge(s_v2a, 16)
            act.activation(st2[:, :], st2[:, :], ACT.Sqrt).then_inc(s_a2v, 1)
            act.wait_ge(s_v2a, 17)
            act.activation(H, H, ACT.Relu).then_inc(s_a2v, 1)
            act.wait_ge(s_a2v, 15)
            dense(3)

            regs = [act.alloc_register(f"act_block{k}") for k in range(RING)]

            act.wait_ge(s_adR, 16)

            def logits(g, k):
                act.wait_ge(gat[k], gat_val(3, g))
                b = act.snap(regs[k], min_val=0, max_val=NB - 1)
                act.activation(raw[:, k % 4, :], adrow[:, bass.DynSlice(b * P, P)], ACT.Identity,
                               bias=ering[:, k, D + 1:D + 2]).then_inc(raw_rdy, 1)

            def weights(g, k):
                act.wait_ge(xrd, g * RING + (k + 1))
                act.activation(sel[:, k % 4, :], pre[:, k % 4, :], ACT.Exp).then_inc(prd, 1)

            def rescale(g, k):
                act.wait_ge(dfr, g * RING + (k + 1))
                act.activation(fac[:, k:k + 1], df[:, k:k + 1], ACT.Exp).then_inc(frd, 1)

            with act.Fori(0, ITERS) as g:
                act.load(regs, brow[0:1, bass.DynSlice(g * RING, RING)])
                lagged(RING, (0, lambda k: logits(g, k)), (2, lambda k: weights(g, k)), (2, lambda k: rescale(g, k)))
            act.wait_ge(s_v2a, 19)
            act.activation(A, H, ACT.Tanh).then_inc(s_a2v, 1)

        @block.vector
        def _(dve):
            n = [0]

            def link(ins):
                n[0] += 1
                ins.then_inc(s_dch, 1)
                dve.wait_ge(s_dch, n[0])

            full = [P, NB, D]

            def over_f(c):
                return c.unsqueeze(2).broadcast_to(full)

            def over_b(r):
                return r.unsqueeze(1).broadcast_to(full)

            dve.wait_ge(s_in, 16)
            dve.tensor_copy(bcast_src[0:1, 0:TR], cmp[0:1, 0:TR].bitcast(I32)).then_inc(s_dp, 1)
            dve.wait_ge(s_io, 15)
            dve.wait_ge(s_pp, 1)
            q = TR // 4
            for i in range(4):
                ins = dve.tensor_scalar(cmp[:, i * q:(i + 1) * q], PS[:, i, 0:q], col[:, 1:2], None, ALU.is_lt)
            link(ins)
            link(dve.reduce_sum(col[:, 2:3], cmp[:, 0:TR], axis=AX))
            link(dve.tensor_tensor(col[:, 2:3], col[:, 2:3], col[:, 0:1], ALU.add))
            dve.tensor_scalar(reach, reach, col[:, 2:3], None, ALU.is_gt).then_inc(s_dp, 1)
            dve.wait_ge(s_pp, 2)
            link(dve.tensor_copy(bcol[:, :], PS[:, 4, 0:SCH]))
            q = SW // 4
            for i in range(4):
                ins = dve.tensor_copy(brow[:, i * q:(i + 1) * q], PS[0:1, (5, 6, 7, 0)[i], 0:q])
            link(ins)
            link(dve.tensor_tensor(tcol[:, :], scol[:, :], bcol[:, :], ALU.subtract))
            dve.tensor_copy(ti[:, :], tcol[:, :]).then_inc(s_dp, 1)
            dve.wait_ge(s_io, 15)
            for i in range(4):
                link(dve.tensor_scalar(bcast_src[0:1, i * q:(i + 1) * q], PS[0:1, (5, 6, 7, 0)[i], 0:q], -1.0, None, ALU.mult))
            link(dve.tensor_tensor(bcast_src[0:1, 0:SW], bcast_src[0:1, 0:SW], srow[0:1, 0:SW], ALU.add))
            link(dve.tensor_copy(trow[:, :], bcast_src[0:1, 0:SW]))
            link(dve.tensor_scalar(bcol[:, :], bcol[:, :], float(P), None, ALU.mult))
            dve.wait_ge(s_er, 16 * 3 * SCH)
            for c in range(SCH):
                dve.tensor_copy(erow[0][:, c, :], erow[0][:, c, :].bitcast(I32))
                ins = dve.tensor_scalar(erow[1][:, c, :], erow[1][:, c, :].bitcast(I32), bcol[:, c:c + 1], None, ALU.subtract)
            ins.then_inc(s_dp, 1)
            for i in range(3 * SCH):
                dve.wait_ge(s_pp, 2 + i + 1)
                t = (idx, dstl, wst)[i % 3]
                dve.tensor_copy(t[:, i // 3 * P:(i // 3 + 1) * P], PS[:, i % 8, 0:P]).then_inc(s_dp, 1)
            dve.wait_ge(s_w, 16 * 18)
            dve.wait_ge(s_pp, 2 + 3 * SCH + 1)
            dve.memset(w4x[:, D:D + 1], 0.0)
            dve.tensor_copy(w4x[:, D + 1:D + 3], PS[0:D, 0, 0:2])
            dve.memset(col[:, 3:4], SOFT_EPS)
            link(dve.tensor_scalar(col[:, 4:5], col[:, 0:1], float(z.LAST), None, ALU.is_lt))

            def norm(v, a):
                link(dve.reduce_sum(st1[:, :], X[:, :, :], axis=AX))
                link(dve.tensor_scalar(st1[:, :], st1[:, :], 1.0 / D, None, ALU.mult))
                dve.tensor_tensor(H, X[:, :, :], over_f(st1[:, :]), ALU.subtract).then_inc(s_v2a, 1)
                dve.wait_ge(s_a2v, a)
                link(dve.reduce_sum(st2[:, :], A, axis=AX))
                dve.tensor_scalar(st2[:, :], st2[:, :], 1.0 / D, LN_EPS, ALU.mult, ALU.add).then_inc(s_v2a, 1)
                dve.wait_ge(s_a2v, a + 1)
                link(dve.reciprocal(st2[:, :], st2[:, :]))
                dve.tensor_tensor(H, H, over_f(st2[:, :]), ALU.mult).then_inc(s_v2a, 1)
                dve.wait_ge(s_a2v, a + 2)

            def dense(d):
                def turned_copy(g, i):
                    dve.wait_ge(d_tr, g * DU + (d * NB + i + 5))
                    w = 2 * P if d == 0 else P
                    dve.tensor_copy(tT[:, i % 4, 0:w], PS[0:D, i % 2, 0:w]).then_inc(d_tc, 1)

                def finish(g, i):
                    b = g * DU + i
                    if d == 1:
                        dve.wait_ge(d_m2, g * DU + (i + 1))
                        dve.tensor_copy(H[:, bass.DynSlice(b, 1), :].rearrange("p a f -> p (a f)"), PS[:, 4 + i % 4, 0:D]).then_inc(d_po, 1)
                        return
                    dve.wait_ge(d_m1, g * DU + (d * NB + i + 1))
                    if d == 3:
                        dve.tensor_copy(A3[:, bass.DynSlice(b, 1), :].rearrange("p a f -> p (a f)"), PS[:, 2 + i % 2, 0:D + 2])
                        dve.tensor_copy(adc[:, bass.DynSlice(b, 1)], PS[:, 2 + i % 2, D + 2:D + 3]).then_inc(d_po, 1)
                    else:
                        xb = X[:, bass.DynSlice(b, 1), :].rearrange("p a f -> p (a f)")
                        dve.tensor_tensor(xb, xb, PS[:, 2 + i % 2, 0:D], ALU.add).then_inc(d_po, 1)

                with dve.Fori(0, NB // DU) as g:
                    lagged(DU, (3 if d == 1 else 2, lambda i: finish(g, i)), (0, lambda i: turned_copy(g, i)))
                dve.wait_ge(d_po, (d + 1) * NB)

            regs = [dve.alloc_register(f"dve_block{k}") for k in range(RING)]

            def steps(L):
                base, add_base = L * STEPS, L * (STEPS + 1) + 1
                acc, W = ((A, D), (A, D), (A2, 2 * D))[L]

                def one_hot(g, k):
                    s = g * RING + k
                    if L == 0:
                        dve.tensor_scalar(sel[:, k % 4, :], iota[:, :], dstl[:, bass.DynSlice(s, 1)], wst[:, bass.DynSlice(s, 1)],
                                          ALU.is_equal, ALU.mult).then_inc(sel_rdy, 1)
                    else:
                        dve.tensor_scalar(sel[:, k % 4, :], iota[:, :], dstl[:, bass.DynSlice(s, 1)], None,
                                          ALU.is_equal).then_inc(sel_rdy, 1)

                def pre_message(g, k):
                    dve.wait_ge(ea_mm, g * RING + (k + 1))
                    dve.wait_ge(gat[k], gat_val(L, g))
                    dve.tensor_tensor(pre[:, k % 4, 0:D], ering[:, k, 0:D], PS[:, 4 + k % 4, 0:D], ALU.add).then_inc(pre_rdy, 1)

                def add(g, k):
                    b = dve.snap(regs[k], min_val=0, max_val=NB - 1)
                    ab = acc[:, bass.DynSlice(b, 1), :].rearrange("p a f -> p (a f)")
                    dve.wait_ge(slot_free, g * RING + (base + RING + k + 1))
                    dve.wait_ge(added, g * RING + (add_base + k))
                    dve.tensor_tensor(ab, ab, PS[:, k % 4, 0:W], ALU.add).then_inc(added, 1)

                dve.memset(acc, 0.0).then_inc(added, 1)
                with dve.Fori(0, ITERS) as g:
                    dve.load(regs, brow[0:1, bass.DynSlice(g * RING, RING)])
                    if L == 1:
                        lagged(RING, (0, lambda k: one_hot(g, k)), (0, lambda k: pre_message(g, k)), (3, lambda k: add(g, k)))
                    else:
                        lagged(RING, (0, lambda k: one_hot(g, k)), (2, lambda k: add(g, k)))
                dve.wait_ge(added, add_base + STEPS)

            norm(0, 1)
            dve.sem_inc(tab_ready[0], 1)
            steps(0)
            dense(0)
            link(dve.memset(eatt[DE:DE + 1, :, :], 1.0))
            norm(3, 4)
            dve.sem_inc(tab_ready[1], 1)
            steps(1)
            dve.tensor_tensor(H, H, A, ALU.add).then_inc(s_v2a, 1)
            dense(1)
            link(dve.tensor_scalar(H[:, NB - 1, :], H[:, NB - 1, :], col[:, 4:5], None, ALU.mult))
            dve.reduce_sum(bs[:, 0, :], H.rearrange("p b f -> p f b"), axis=AX).then_inc(s_bnp, 1)
            dve.wait_ge(s_bnp, 2)
            link(dve.tensor_scalar(bs[:, 2, :], PS[:, 0, 0:D], 1.0 / z.N, None, ALU.mult))
            link(dve.tensor_tensor(H, H, over_b(bs[:, 2, :]), ALU.subtract))
            dve.tensor_scalar(H[:, NB - 1, :], H[:, NB - 1, :], col[:, 4:5], None, ALU.mult).then_inc(s_v2a, 1)
            dve.wait_ge(s_a2v, 7)
            dve.reduce_sum(bs[:, 1, :], A.rearrange("p b f -> p f b"), axis=AX).then_inc(s_bnp, 1)
            dve.wait_ge(s_bnp, 4)
            dve.tensor_scalar(bs[:, 1, :], PS[:, 1, 0:D], 1.0 / z.N, BN_EPS, ALU.mult, ALU.add).then_inc(s_v2a, 1)
            dve.wait_ge(s_a2v, 8)
            link(dve.reciprocal(bs[:, 1, :], bs[:, 1, :]))
            link(dve.tensor_tensor(bs[:, 1, :], bs[:, 1, :], bn[:, 0, :], ALU.mult))
            link(dve.tensor_tensor(H, H, over_b(bs[:, 1, :]), ALU.mult))
            dve.tensor_tensor(H, H, over_b(bn[:, 1, :]), ALU.add).then_inc(s_v2a, 1)
            dve.wait_ge(s_a2v, 9)
            link(dve.tensor_tensor(X[:, :, :], X[:, :, :], H, ALU.add))
            norm(11, 10)
            link(dve.tensor_scalar(A2[:, :, D:2 * D], H, SOFT_EPS, None, ALU.add))
            link(dve.tensor_tensor(A2[:, :, D:2 * D], A2[:, :, D:2 * D], A2[:, :, 0:D], ALU.mult))
            dve.sem_inc(tab_ready[2], 1)
            dve.wait_ge(tab_wr[2], 16)
            steps(2)
            link(dve.tensor_scalar(A2[:, :, 0:D], A2[:, :, 0:D], 1.0, None, ALU.max))
            link(dve.reciprocal(A2[:, :, 0:D], A2[:, :, 0:D]))
            link(dve.tensor_tensor(A2[:, :, 0:D], A2[:, :, 0:D], A2[:, :, D:2 * D], ALU.mult))
            dve.tensor_tensor(H, H, A2[:, :, 0:D], ALU.add).then_inc(s_v2a, 1)
            dense(2)
            norm(15, 13)
            dense(3)
            add_base = 3 * (STEPS + 1) + 1
            dve.memset(A3[:, :, D:D + 1], 1.0).then_inc(added, 1)
            dve.wait_ge(added, add_base)
            dve.sem_inc(tab_ready[3], 1)
            dve.tensor_tensor(lc[:, :], A3[:, :, D + 1:D + 2].rearrange("p b a -> p (b a)"), adc[:, :], ALU.add).then_inc(s_v2a, 1)
            dve.wait_ge(s_v2a, 18)
            link(dve.scalar_tensor_tensor(out=lc[:, :], in0=lc[:, :], scalar=SLOPE, in1=lc[:, :], op0=ALU.mult, op1=ALU.max))
            dve.wait_ge(s_adT, 1)
            dve.tensor_copy(adT[:, :], PS[0:NB, 6, 0:P]).then_inc(s_adS, 1)
            dve.wait_ge(tab_wr[3], 16)

            base = 3 * STEPS

            def off_block(g, k):
                dve.tensor_scalar(zb[:, k % 4, :], iobf[:, :], dstl[:, bass.DynSlice(g * RING + k, 1)], -BIG,
                                  ALU.not_equal, ALU.mult).then_inc(z_rdy, 1)

            def leaky(g, k):
                dve.wait_ge(raw_rdy, g * RING + (k + 1))
                dve.scalar_tensor_tensor(out=msg[:, k % 4, :], in0=raw[:, k % 4, :], scalar=SLOPE, in1=raw[:, k % 4, :],
                                         op0=ALU.mult, op1=ALU.max).then_inc(u_rdy, 1)

            def tile_max(g, k):
                dve.wait_ge(psa, g * RING + (k + 1))
                dve.reduce_max(cm[:, k:k + 1], PS[:, k % 2, 0:P], axis=AX).then_inc(cmx, 1)

            def new_max(g, k):
                b = dve.snap(regs[k], min_val=0, max_val=NB - 1)
                dve.wait_ge(cmx, g * RING + (k + 1))
                dve.tensor_tensor(ln_[:, k:k + 1], cm[:, k:k + 1], lc[:, bass.DynSlice(b, 1)], ALU.max).then_inc(lcn, 1)

            def shifted(g, k):
                dve.wait_ge(psc, g * RING + (k + 1))
                dve.tensor_tensor(pre[:, k % 4, :], msg[:, k % 4, :], PS[:, 2 + k % 2, 0:P], ALU.subtract).then_inc(xrd, 1)

            def drop(g, k):
                b = dve.snap(regs[k], min_val=0, max_val=NB - 1)
                dve.wait_ge(lcn, g * RING + (k + 1))
                dve.tensor_tensor(df[:, k:k + 1], lc[:, bass.DynSlice(b, 1)], ln_[:, k:k + 1], ALU.subtract).then_inc(dfr, 1)

            def store_max(g, k):
                b = dve.snap(regs[k], min_val=0, max_val=NB - 1)
                dve.wait_ge(dfr, g * RING + (k + 1))
                dve.tensor_copy(lc[:, bass.DynSlice(b, 1)], ln_[:, k:k + 1]).then_inc(lcs, 1)

            def add_scaled(g, k):
                b = dve.snap(regs[k], min_val=0, max_val=NB - 1)
                ab = A3[:, bass.DynSlice(b, 1), 0:D + 1].rearrange("p a f -> p (a f)")
                dve.wait_ge(added, g * RING + (add_base + k))
                dve.wait_ge(frd, g * RING + (k + 1))
                dve.wait_ge(slot_free, g * RING + (base + RING + k + 1))
                dve.scalar_tensor_tensor(out=ab, in0=ab, scalar=fac[:, k:k + 1], in1=PS[:, 4 + k % 2, 0:D + 1],
                                         op0=ALU.mult, op1=ALU.add).then_inc(added, 1)

            with dve.Fori(0, ITERS) as g:
                dve.load(regs, brow[0:1, bass.DynSlice(g * RING, RING)])
                lagged(RING, (0, lambda k: off_block(g, k)), (0, lambda k: leaky(g, k)), (1, lambda k: tile_max(g, k)), (4, lambda k: add_scaled(g, k)),
                       (1, lambda k: new_max(g, k)), (2, lambda k: shifted(g, k)), (1, lambda k: drop(g, k)),
                       (1, lambda k: store_max(g, k)))
            dve.wait_ge(added, add_base + STEPS)
            den = A3[:, :, D:D + 1].rearrange("p b a -> p (b a)")
            link(dve.tensor_scalar(st1[:, :], den, GAT_EPS, None, ALU.add))
            link(dve.reciprocal(st1[:, :], st1[:, :]))
            link(dve.tensor_tensor(H, A3[:, :, 0:D], over_f(st1[:, :]), ALU.mult))
            dve.tensor_tensor(H, H, over_b(bn[:, 2, :]), ALU.add).then_inc(s_v2a, 1)
            dve.wait_ge(s_a2v, 16)
            dve.tensor_tensor(X[:, :, :], X[:, :, :], A, ALU.add).then_inc(s_fin, 1)


def kernel(x, src, dst, edge_attr_32, edge_weight, L0_gnn_mlp_w, L0_gnn_mlp_b, L1_gnn_We, L1_gnn_be, L1_gnn_W1,
           L1_gnn_b1, L1_gnn_W2, L1_gnn_b2, L1_gnn_gamma, L1_gnn_beta, L2_gnn_W, L2_gnn_b, L3_gnn_W,
           L3_gnn_att_src, L3_gnn_att_dst, L3_gnn_bias):
    import concourse.bacc as bacc
    from concourse.bass_utils import run_bass_kernel_spmd as run

    z = Sizes(x.shape[0], src.shape[0])

    def rows(a, fill):
        a = np.asarray(a)
        full = np.full((z.TR * P,) + a.shape[1:], fill, a.dtype)
        full[:a.shape[0]] = a
        return full.reshape((z.TR, P) + a.shape[1:])

    arrays = {
        "x": np.asarray(x), "src": rows(src, 0), "dst": rows(dst, NO_NODE), "ew": rows(edge_weight, 0),
        "eaT": rows(edge_attr_32, 0).transpose(0, 2, 1),
        "w0T": np.asarray(L0_gnn_mlp_w).T, "b0": L0_gnn_mlp_b, "We": L1_gnn_We, "be": L1_gnn_be, "W1": L1_gnn_W1,
        "b1": L1_gnn_b1, "W2": L1_gnn_W2, "b2": L1_gnn_b2, "gamma": L1_gnn_gamma, "beta": L1_gnn_beta,
        "W3": L2_gnn_W, "b3": L2_gnn_b, "W4": L3_gnn_W, "W4T": np.asarray(L3_gnn_W).T,
        "att": np.stack([np.asarray(L3_gnn_att_src), np.asarray(L3_gnn_att_dst)], axis=1), "bias4": L3_gnn_bias,
    }
    arrays = {k: np.ascontiguousarray(a) for k, a in arrays.items()}
    nc = bacc.Bacc("TRN2", target_bir_lowering=False, num_devices=1)
    aps = {k: nc.dram_tensor(f"in_{k}", a.shape, mybir.dt.from_np(a.dtype), kind="ExternalInput").ap()
           for k, a in arrays.items()}
    out = nc.dram_tensor("out_0", tuple(x.shape), F32, kind="ExternalOutput").ap()
    build(nc, z, out=out, **aps)
    r = run(nc, [{f"in_{k}": a for k, a in arrays.items()}], core_ids=[0])
    return r.results[0]["out_0"]
```

```python
from contextlib import ExitStack

import numpy as np

import concourse.bass as bass
from concourse import mybir

F32 = mybir.dt.float32
BF16 = mybir.dt.bfloat16
I32 = mybir.dt.int32
ALU = mybir.AluOpType
ACT = mybir.ActivationFunctionType
AX = mybir.AxisListType.X
P = 128
D = 96
DE = 32
RING = 16
HALF = RING // 2
NO_NODE = 1 << 20
BIG = 2.0 ** 100
LN_EPS = 1e-5
BN_EPS = 1e-5
SOFT_EPS = 1e-7
GAT_EPS = 1e-16
SLOPE = 0.2


class Sizes:
    def __init__(self, nodes, edges):
        self.N, self.E = nodes, edges
        self.NB = -(-nodes // P)
        self.NB += self.NB % 2
        self.LAST = nodes - (self.NB - 1) * P
        self.TILES = -(-edges // P)
        self.ITERS = -(-(self.TILES + self.NB - 1) // RING)
        self.STEPS = self.ITERS * RING
        self.SCH = -(-self.STEPS // P)
        self.SW = self.SCH * P
        rows = max(self.TILES, self.SW - self.NB + 1)
        self.TR = rows + (-rows) % 4
        self.DU = max(u for u in range(2, 17, 2) if self.NB % u == 0)
        assert self.LAST > 0 and D * self.NB >= RING * P + self.SW and 2 * D * self.NB >= self.TR + 7 * self.SW and self.STEPS % 4 == 0 and self.STEPS // 4 <= 512 and self.TR // 4 <= 512


def build(nc, z, x, src, dst, ew, eaT, w0T, b0, We, be, W1, b1, W2, b2, gamma, beta, W3, b3, W4, W4T, att, bias4, out):
    NB, SCH, SW, STEPS, ITERS, TR, DU = z.NB, z.SCH, z.SW, z.STEPS, z.ITERS, z.TR, z.DU
    ctx = ExitStack()
    with ctx:
        def sb(name, shape, dt=F32):
            return ctx.enter_context(nc.sbuf_tensor(name, shape, dt))

        def sem(name):
            return ctx.enter_context(nc.semaphore(name))

        tab = [nc.dram_tensor(f"table{i}", (NB * P, w), F32).ap() for i, w in enumerate((D, D, 2 * D, D + 2))]
        new_dram = nc.dram_tensor("new_block_dram", (1, SW), F32).ap()
        ad_dram = nc.dram_tensor("ad_dram", (NB, P), F32).ap()

        X = sb("X", [P, NB, D])
        R = sb("R", [P, NB * 3 * D])
        H = R[:, 2 * D * NB:3 * D * NB].rearrange("p (b f) -> p b f", f=D)
        A = R[:, 0:D * NB].rearrange("p (b f) -> p b f", f=D)
        A2 = R[:, 0:2 * D * NB].rearrange("p (b f) -> p b f", f=2 * D)
        A3 = R[:, 0:(D + 2) * NB].rearrange("p (b f) -> p b f", f=D + 2)
        adrow = R[:, (D + 2) * NB:(D + 2 + P) * NB]
        cmp = R[:, 0:TR]
        reach = R[:, TR:TR + SW]
        srow = R[:, TR + 4 * SW:TR + 5 * SW]
        bcast_src = R[:, TR + 5 * SW:TR + 5 * SW + max(TR, SW)]
        erow = [R[:, TR + SW + i * SW:TR + SW + (i + 1) * SW].rearrange("p (c e) -> p c e", e=P) for i in range(3)]
        ering = sb("gathered_rows", [P, RING, 2 * D])
        work = sb("work", [P, 8 * D + 12 * P])
        raw, msg, pre, sel = (work[:, i * 4 * P:(i + 1) * 4 * P].rearrange("p (r e) -> p r e", r=4) for i in range(4))
        logit = work[:, 4 * P:12 * P].rearrange("p (r e) -> p r e", r=8)
        stg = work[:, 0:8 * D].rearrange("p (r f) -> p r f", r=4)
        tT = work[0:D, 8 * D:8 * D + 8 * P].rearrange("p (r n) -> p r n", r=4)
        rT = work[0:D, 8 * D + 8 * P:8 * D + 12 * P].rearrange("p (r n) -> p r n", r=4)
        zb = sb("off_block", [P, 8, P], BF16)
        eatt = R[0:DE + 1, D * NB:D * NB + RING * P].rearrange("p (k e) -> p k e", k=RING)
        ib = sb("staged_index", [P, RING], I32)
        idx = sb("src_of_step", [P, SW], I32)
        dstl = sb("dst_in_block", [P, SW])
        wst = sb("weight_of_step", [P, SW])
        brow = sb("block_of_step", [1, SW], I32)
        trow = R[0:1, 2 * D * NB - SW:2 * D * NB].bitcast(I32)
        iota = sb("iota", [P, P])
        ident = sb("ident", [P, P])
        ones = sb("ones", [P, P])
        col = sb("cols", [P, 16])
        scol = sb("step_col", [P, SCH])
        bcol = sb("block_col", [P, SCH])
        tcol = sb("tile_col", [P, SCH])
        ti = sb("tile_idx", [P, SCH], I32)
        st1 = sb("ln_mean", [P, NB])
        st2 = sb("ln_rstd", [P, NB])
        w0 = sb("w0", [D, 2, D])
        wew = sb("we", [DE + 1, D])
        w1 = sb("w1", [D, D])
        w2 = sb("w2", [D, D])
        w3 = sb("w3", [D, D])
        w4x = sb("w4x", [D, D + 3])
        w4t = sb("w4t", [D, D])
        att2 = sb("att2", [D, 2])
        b1c = sb("b1c", [D, 1])
        brows = sb("bias_rows", [1, 3, D])
        bn = sb("bn_rows", [P, 3, D])
        bs = sb("bn_stats", [P, 3, D])
        adc = sb("ad_col", [P, NB])
        adT = sb("ad_T", [NB, P])
        lc = sb("run_max", [P, NB])
        cm = sb("tile_max", [P, RING])
        ln_ = sb("new_max", [P, RING])
        old = sb("old_max", [P, RING])
        fac = sb("rescale", [P, RING])
        PS = ctx.enter_context(nc.psum_tensor("PS", [P, 8, 512], F32))

        s_in = sem("inputs_loaded")
        s_w = sem("weights_loaded")
        s_io = sem("pool_consts")
        s_dp = sem("dve_prep")
        s_pp = sem("pe_prep")
        s_er = sem("edge_rows_gathered")
        s_dch = sem("dve_chain")
        s_ach = sem("act_chain")
        s_v2a = sem("dve_to_act")
        s_a2v = sem("act_to_dve")
        s_bnp = sem("bn_summed")
        tab_ready = [sem(f"table_values{i}") for i in range(4)]
        tab_wr = [sem(f"table_written{i}") for i in range(4)]
        staged = [sem(f"index_staged{h}") for h in range(2)]
        gat = [sem(f"gathered{k}") for k in range(RING)]
        eah = [sem(f"edge_features_loaded{k}") for k in range(RING)]
        slot_free = sem("slot_free")
        sel_rdy = sem("one_hot_ready")
        added = sem("block_added")
        ea_mm = sem("edge_product_ready")
        pre_rdy = sem("pre_message_ready")
        msg_rdy = sem("message_ready")
        raw_rdy = sem("raw_logits_ready")
        u_rdy = sem("logits_ready")
        oldr = sem("old_max_ready")
        z_rdy = sem("off_block_ready")
        psa = sem("logits_turned")
        cmx = sem("tile_max_ready")
        s_nb = sem("new_block_row_ready")
        s_nbd = sem("new_block_row_in_dram")
        s_nbl = sem("new_block_rows_loaded")
        lcn = sem("new_max_ready")
        psc = sem("max_rows_ready")
        xrd = sem("shifted_ready")
        prd = sem("weights_ready")
        d_st = sem("dense_staged")
        d_tr = sem("dense_turned")
        d_tc = sem("dense_turned_copied")
        d_m1 = sem("dense_product1")
        d_re = sem("dense_relu")
        d_m2 = sem("dense_product2")
        d_po = sem("dense_done")
        s_adT = sem("ad_turned")
        s_adS = sem("ad_copied")
        s_adD = sem("ad_in_dram")
        s_adR = sem("ad_rows_loaded")
        s_fin = sem("result_ready")
        s_out = sem("result_stored")

        block = ctx.enter_context(nc.Block())

        def gat_val(L, g):
            return g * 16 + (16 * (L * ITERS) + 16)

        def half_bank(bank, k):
            return PS[:, bank + k // 2 % 2, k % 2 * P:(k % 2 + 1) * P]

        def lagged(n, *stages):
            top = max(l for l, _ in stages)
            for i in range(n + top):
                for lag, fn in stages:
                    if 0 <= i - lag < n:
                        fn(i - lag)

        def pipelined(eng, *stages, load=None):
            top = max(s[0] for s in stages)
            earliest = min(s[0] for s in stages)

            def issue(g, first, limit):
                for lag, fn, *pair in stages:
                    c = first - lag
                    if 0 <= c < limit and (not pair or c % 2 == 1):
                        if lag == earliest and load is not None and c % HALF == 0:
                            load(g + c // RING, c % RING)
                        fn(g + c // RING, c % RING)

            for i in range(top):
                issue(0, i, STEPS)
            with eng.Fori(0, ITERS - 1) as g:
                for j in range(RING):
                    issue(g, top + j, STEPS)
            for j in range(RING):
                issue(ITERS - 1, top + j, RING)

        @block.sync
        def _(sp):
            with nc.allow_non_contiguous_dma(reason="one destination per tile"):
                sp.dma_start(cmp[0:1, 0:TR].bitcast(I32), dst[:, P - 1:P].rearrange("t a -> a t")).then_inc(s_in, 16)
            sp.wait_ge(s_io, 1)
            sp.dma_start(X[:, 0:NB - 1, :], x[0:(NB - 1) * P, :].rearrange("(b p) f -> p b f", p=P)).then_inc(s_w, 16)
            sp.dma_start(X[0:z.LAST, NB - 1, :], x[(NB - 1) * P:z.N, :]).then_inc(s_w, 16)
            sp.dma_start(w0[:, :, :], w0T.rearrange("(h i) o -> i h o", h=2)).then_inc(s_w, 16)
            sp.dma_start(wew[0:DE, :], We).then_inc(s_w, 16)
            sp.dma_start(wew[DE:DE + 1, :], be.rearrange("(a n) -> a n", a=1)).then_inc(s_w, 16)
            for t, s in ((w1, W1), (w2, W2), (w3, W3), (w4t, W4T)):
                sp.dma_start(t[:, :], s).then_inc(s_w, 16)
            sp.dma_start(w4x[:, 0:D], W4).then_inc(s_w, 16)
            sp.dma_start(att2[:, :], att).then_inc(s_w, 16)
            sp.dma_start(b1c[:, :], b1.rearrange("(n a) -> n a", a=1)).then_inc(s_w, 16)
            for i, s in enumerate((b0, b2, b3)):
                sp.dma_start(brows[:, i, :], s.rearrange("(a n) -> a n", a=1)).then_inc(s_w, 16)
            for i, s in enumerate((gamma, beta, bias4)):
                sp.dma_start(bn[:, i, :], s.rearrange("(a n) -> a n", a=1).broadcast_to([P, D])).then_inc(s_w, 16)

            sp.wait_ge(s_nb, 1)
            sp.dma_start(new_dram, bcast_src[0:1, 0:SW]).then_inc(s_nbd, 16)
            sp.wait_ge(s_nbd, 16)
            def stage_indices(L, g):
                for h in range(2):
                    if L > 0 or not isinstance(g, int):
                        for k in range(h * HALF, (h + 1) * HALF):
                            sp.wait_ge(gat[k], g * 16 + 16 * L * ITERS)
                    sp.dma_start(ib[:, h * HALF:(h + 1) * HALF], idx[:, bass.DynSlice(g * RING + h * HALF, HALF)])\
                        .then_inc(staged[h], 16)

            for L in range(4):
                if L == 0:
                    sp.wait_ge(s_dp, 4 + 3 * SCH)
                stage_indices(L, 0)
                sp.wait_ge(tab_ready[L], 1)
                vals = (H, H, A2, A3)[L]
                sp.dma_start(tab[L].rearrange("(b p) f -> p b f", p=P), vals).then_inc(tab_wr[L], 16)
                if L == 1:
                    sp.dma_start(wst[:, :], new_dram.broadcast_to([P, SW])).then_inc(s_nbl, 16)
                if L == 3:
                    sp.wait_ge(s_adS, 1)
                    sp.dma_start(ad_dram, adT[:, :]).then_inc(s_adD, 16)
                    sp.wait_ge(s_adD, 16)
                    sp.dma_start(adrow, ad_dram.rearrange("(a b) p -> a (b p)", a=1).broadcast_to([P, NB * P]))\
                        .then_inc(s_adR, 16)
                with sp.Fori(1, ITERS) as g:
                    stage_indices(L, g)
            sp.wait_ge(s_fin, 1)
            sp.dma_start(out[0:(NB - 1) * P, :].rearrange("(b p) f -> p b f", p=P), X[:, 0:NB - 1, :]).then_inc(s_out, 16)
            sp.dma_start(out[(NB - 1) * P:z.N, :], X[0:z.LAST, NB - 1, :]).then_inc(s_out, 16)
            sp.wait_ge(s_out, 32)

        @block.gpsimd
        def _(pool):
            pool.memset(X[:, NB - 1, :], 0.0).then_inc(s_io, 1)
            pool.iota(iota[:, :], pattern=[[1, P]], base=0, channel_multiplier=0, allow_small_or_imprecise_dtypes=True).then_inc(s_io, 1)
            pool.iota(reach, pattern=[[1, SW]], base=0, channel_multiplier=0, allow_small_or_imprecise_dtypes=True).then_inc(s_io, 1)
            pool.iota(srow[0:1, :], pattern=[[1, SW]], base=0, channel_multiplier=0, allow_small_or_imprecise_dtypes=True).then_inc(s_io, 1)
            pool.iota(scol[:, :], pattern=[[P, SCH]], base=0, channel_multiplier=1, allow_small_or_imprecise_dtypes=True).then_inc(s_io, 1)
            pool.iota(col[:, 0:1], pattern=[[0, 1]], base=0, channel_multiplier=1, allow_small_or_imprecise_dtypes=True).then_inc(s_io, 1)
            pool.iota(col[:, 1:2], pattern=[[0, 1]], base=P, channel_multiplier=P, allow_small_or_imprecise_dtypes=True).then_inc(s_io, 1)
            pool.memset(ones[:, :], 1.0).then_inc(s_io, 1)
            pool.memset(ident[:, :], 0.0).then_inc(s_io, 1)
            pool.wait_ge(s_io, 9)
            pool.affine_select(out=ident[:, :], in_=ident[:, :], compare_op=ALU.not_equal, fill=1.0, base=0,
                               pattern=[[-1, P]], channel_multiplier=1).then_inc(s_io, 1)
            pool.wait_ge(s_dp, 3)
            for c in range(SCH):
                for r, t in zip(erow, (src, dst, ew)):
                    o = r[:, c, :] if t is ew else r[:, c, :].bitcast(I32)
                    pool.indirect_dma_start(o, None, t, bass.IndirectOffsetOnAxis(ap=ti[:, c:c + 1], axis=0))\
                        .then_inc(s_er, 16)
            for L in range(4):
                pool.wait_ge(tab_wr[L], 16)
                W = (D, D, 2 * D, D + 2)[L]
                few = (4, 4, 4, 2)[L]
                with pool.Fori(0, ITERS) as g:
                    for h in range(2):
                        pool.wait_ge(staged[h], g * 16 + (16 * (L * ITERS) + 16))
                        pool.nop(nofuse=True)
                        for k in range(h * HALF, (h + 1) * HALF):
                            if k % few == 0:
                                pool.wait_ge(slot_free, g * RING + (L * STEPS + k + few))
                                pool.nop(nofuse=True)
                            pool.indirect_dma_start(ering[:, k, 0:W], None, tab[L],
                                                    bass.IndirectOffsetOnAxis(ap=ib[:, k:k + 1], axis=0)).then_inc(gat[k], 16)

        @block.tensor
        def _(pe):
            pe.sem_inc(slot_free, RING)
            pe.sem_inc(d_tr, 4)
            pe.sem_inc(prd, 8)
            pe.wait_ge(s_io, 10)
            pe.wait_ge(s_dp, 1)
            q = TR // 4
            for i in range(4):
                last = pe.matmul(PS[:, i, 0:q], ones[0:1, :], bcast_src[0:1, i * q:(i + 1) * q], start=True, stop=True)
            last.then_inc(s_pp, 1)
            pe.wait_ge(s_dp, 2)
            for c in range(SCH):
                pe.matmul(PS[:, 4, c:c + 1], reach[0:NB - 1, c * P:(c + 1) * P], ones[0:NB - 1, 0:1], start=True, stop=True)
            q = SW // 4
            for i in range(4):
                last = pe.matmul(PS[0:1, (5, 6, 7, 0)[i], 0:q], ones[0:NB - 1, 0:1], reach[0:NB - 1, i * q:(i + 1) * q],
                                 start=True, stop=True)
            last.then_inc(s_pp, 1)
            pe.wait_ge(s_dp, 4)
            for i in range(3 * SCH):
                if i >= 8:
                    pe.wait_ge(s_dp, 4 + i - 7)
                pe.transpose(PS[:, i % 8, 0:P], erow[i % 3][:, i // 3, :], ident[:, :]).then_inc(s_pp, 1)
            pe.wait_ge(s_w, 16 * 18)
            pe.wait_ge(s_dp, 4 + 3 * SCH)
            pe.matmul(PS[0:D, 0, 0:2], w4t[:, :], att2[:, :], start=True, stop=True).then_inc(s_pp, 1)
            base_pp = 2 + 3 * SCH + 1

            def dense(d):
                halves = 2 if d == 0 else 1

                def turn(g, i):
                    pe.wait_ge(d_st, g * DU + (d * NB + i + 1))
                    for q in range(halves):
                        last = pe.transpose(PS[0:D, i % 2, q * P:(q + 1) * P], stg[:, i % 4, q * D:(q + 1) * D], ident[:, :])
                    last.then_inc(d_tr, 1)

                def product1(g, i):
                    pe.wait_ge(d_tc, g * DU + (d * NB + i + 1))
                    o = PS[:, 2 + i % 2, 0:(D + 3 if d == 3 else D)]
                    t = tT[:, i % 4, :]
                    if d == 0:
                        pe.matmul(o, t[:, 0:P], w0[:, 0, :], start=True, stop=False)
                        pe.matmul(o, t[:, P:2 * P], w0[:, 1, :], start=False, stop=False)
                        pe.matmul(o, ones[0:1, :], brows[:, 0, :], start=False, stop=True).then_inc(d_m1, 1)
                    elif d == 1:
                        pe.matmul(PS[0:D, 2 + i % 2, 0:P], w1[:, :], t[:, 0:P], start=True, stop=True).then_inc(d_m1, 1)
                    elif d == 2:
                        pe.matmul(o, t[:, 0:P], w3[:, :], start=True, stop=False)
                        pe.matmul(o, ones[0:1, :], brows[:, 2, :], start=False, stop=True).then_inc(d_m1, 1)
                    else:
                        pe.matmul(o, t[:, 0:P], w4x[:, :], start=True, stop=True).then_inc(d_m1, 1)

                def product2(g, i):
                    pe.wait_ge(d_re, g * DU + (i + 1))
                    o = PS[:, 4 + i % 4, 0:D]
                    pe.matmul(o, rT[:, i % 4, :], w2[:, :], start=True, stop=False)
                    pe.matmul(o, ones[0:1, :], brows[:, 1, :], start=False, stop=True).then_inc(d_m2, 1)

                with pe.Fori(0, NB // DU) as g:
                    stages = [(0, lambda i: turn(g, i)), (1, lambda i: product1(g, i))]
                    if d == 1:
                        stages.append((2, lambda i: product2(g, i)))
                    lagged(DU, *stages)

            def steps(L):
                base = L * STEPS
                W = (D, D, 2 * D)[L]

                def edge_product(g, k):
                    pe.wait_ge(eah[k], g * 16 + 16)
                    pe.matmul(PS[:, 4 + k % 4, 0:D], eatt[:, k, :], wew[:, :], start=True, stop=True).then_inc(ea_mm, 1)

                def sum_tile(g, k):
                    pe.wait_ge(sel_rdy, g * RING + (base + k + 1))
                    if L == 1:
                        pe.wait_ge(msg_rdy, g * RING + (k + 1))
                        rhs = msg[:, k % 4, 0:D]
                    else:
                        pe.wait_ge(gat[k], gat_val(L, g))
                        rhs = ering[:, k, 0:W]
                    pe.matmul(PS[:, k % 4, 0:W], sel[:, k % 4, :], rhs, start=True, stop=True).then_inc(slot_free, 1)

                if L == 1:
                    pipelined(pe, (0, edge_product), (2, sum_tile))
                else:
                    pipelined(pe, (0, sum_tile))

            def attention_steps():
                def turn_logits(g, k):
                    pe.wait_ge(u_rdy, g * RING + (k + 1))
                    for j in (k - 1, k):
                        pe.transpose(half_bank(0, j), logit[:, j % 8, :], ident[:, :]).then_inc(psa, 1)

                def spread_max(g, k):
                    pe.wait_ge(lcn, g * RING + (k + 2))
                    for j in (k - 1, k):
                        pe.transpose(half_bank(2, j), ln_[:, j:j + 1].broadcast_to([P, P]), ident[:, :]).then_inc(psc, 1)

                def sum_tile(g, k):
                    pe.wait_ge(prd, g * RING + (k + 9))
                    pe.wait_ge(gat[k], gat_val(3, g))
                    pe.matmul(PS[:, 4 + k % 4, 0:D + 1], sel[:, k % 4, :], ering[:, k, 0:D + 1], start=True, stop=True)\
                        .then_inc(slot_free, 1)

                pipelined(pe, (10, sum_tile), (3, turn_logits, "pair"), (6, spread_max, "pair"))

            steps(0)
            dense(0)
            steps(1)
            dense(1)
            for i in range(2):
                pe.wait_ge(s_bnp, 2 * i + 1)
                pe.matmul(PS[:, i, 0:D], ones[:, :], bs[:, i, :], start=True, stop=True).then_inc(s_bnp, 1)
            steps(2)
            dense(2)
            dense(3)
            pe.wait_ge(d_po, 4 * NB)
            pe.transpose(PS[0:NB, 6, 0:P], adc[:, :], ident[:, :]).then_inc(s_adT, 1)
            attention_steps()

        @block.scalar
        def _(act):
            n = [0]

            def link(ins):
                n[0] += 1
                ins.then_inc(s_ach, 1)
                act.wait_ge(s_ach, n[0])

            def norm(i):
                act.wait_ge(s_v2a, 3 * i + 1)
                act.activation(A, H, ACT.Square).then_inc(s_a2v, 1)
                act.wait_ge(s_v2a, 3 * i + 2)
                act.activation(st2[:, :], st2[:, :], ACT.Sqrt).then_inc(s_a2v, 1)
                act.wait_ge(s_v2a, 3 * i + 3)
                ins = act.activation(H, H, ACT.Relu)
                ins.then_inc(s_a2v, 1)

            def dense(d):
                def stage(g, i):
                    act.wait_ge(d_tr, g * DU + (d * NB + max(i + 1, 4)))
                    b = g * DU + i
                    if d == 0:
                        act.copy(stg[:, i % 4, 0:D], H[:, bass.DynSlice(b, 1), :].rearrange("p a f -> p (a f)"))
                        act.copy(stg[:, i % 4, D:2 * D], A[:, bass.DynSlice(b, 1), :].rearrange("p a f -> p (a f)")).then_inc(d_st, 1)
                    else:
                        act.copy(stg[:, i % 4, 0:D], H[:, bass.DynSlice(b, 1), :].rearrange("p a f -> p (a f)")).then_inc(d_st, 1)

                def relu(g, i):
                    act.wait_ge(d_m1, g * DU + (d * NB + i + 1))
                    act.activation(rT[:, i % 4, :], PS[0:D, 2 + i % 2, 0:P], ACT.Relu, bias=b1c[:, 0:1]).then_inc(d_re, 1)

                with act.Fori(0, NB // DU) as g:
                    if d == 1:
                        lagged(DU, (0, lambda i: stage(g, i)), (1, lambda i: relu(g, i)))
                    else:
                        lagged(DU, (0, lambda i: stage(g, i)))

            norm(0)
            act.wait_ge(added, 1 + STEPS)
            dense(0)
            norm(1)

            def relu_message(g, k):
                act.wait_ge(pre_rdy, g * RING + (k + 1))
                act.activation(msg[:, k % 4, 0:D], pre[:, k % 4, 0:D], ACT.Relu).then_inc(msg_rdy, 1)

            tregs = [act.alloc_register(f"tile{k}") for k in range(RING)]

            def load_edge_features(g, k):
                if k % HALF == 0:
                    act.load(tregs[k:k + HALF], trow[0:1, bass.DynSlice(g * RING + k, HALF)])
                t = act.snap(tregs[k], min_val=0, max_val=TR - 1)
                act.dma_start(eatt[0:DE, k, :], eaT[bass.DynSlice(t, 1), :, :].rearrange("a f e -> (a f) e")).then_inc(eah[k], 16)

            for k in range(RING):
                load_edge_features(0, k)
            pipelined(act, (0, relu_message), (-RING, load_edge_features))
            act.wait_ge(s_v2a, 7)
            dense(1)
            act.wait_ge(s_v2a, 8)
            act.activation(A, H, ACT.Square).then_inc(s_a2v, 1)
            act.wait_ge(s_v2a, 9)
            act.activation(bs[:, 1, :], bs[:, 1, :], ACT.Sqrt).then_inc(s_a2v, 1)
            act.wait_ge(s_v2a, 10)
            act.activation(H, H, ACT.Relu).then_inc(s_a2v, 1)
            act.wait_ge(s_v2a, 11)
            act.activation(A, H, ACT.Square).then_inc(s_a2v, 1)
            act.wait_ge(s_v2a, 12)
            act.activation(st2[:, :], st2[:, :], ACT.Sqrt).then_inc(s_a2v, 1)
            act.wait_ge(s_v2a, 13)
            link(act.activation(H, H, ACT.Relu))
            act.activation(A2[:, :, 0:D], H, ACT.Exp, bias=col[:, 3:4]).then_inc(s_a2v, 1)
            act.wait_ge(s_v2a, 14)
            dense(2)
            act.wait_ge(s_v2a, 15)
            act.activation(A, H, ACT.Square).then_inc(s_a2v, 1)
            act.wait_ge(s_v2a, 16)
            act.activation(st2[:, :], st2[:, :], ACT.Sqrt).then_inc(s_a2v, 1)
            act.wait_ge(s_v2a, 17)
            act.activation(H, H, ACT.Relu).then_inc(s_a2v, 1)
            act.wait_ge(s_a2v, 15)
            dense(3)

            act.wait_ge(s_v2a, 19)

            def off_block(g, k):
                act.wait_ge(gat[k], gat_val(3, g))
                act.activation(zb[:, k % 8, :], iota[:, :], ACT.Abs, bias=dstl[:, bass.DynSlice(g * RING + k, 1)],
                               scale=BIG).then_inc(z_rdy, 1)

            def weights(g, k):
                act.wait_ge(xrd, g * RING + (k + 1))
                act.activation(sel[:, k % 4 - 1:k % 4 + 1, :], logit[:, k % 8 - 1:k % 8 + 1, :], ACT.Exp, scale=-1.0).then_inc(prd, 2)

            def rescale(g, k):
                act.wait_ge(lcn, g * RING + (k + 2))
                act.activation(fac[:, k:k + 1], old[:, k:k + 1], ACT.Exp, bias=ln_[:, k:k + 1], scale=-1.0)

            pipelined(act, (0, off_block), (6, rescale), (8, weights, "pair"))
            act.wait_ge(s_v2a, 20)
            act.activation(A, H, ACT.Tanh).then_inc(s_a2v, 1)

        @block.vector
        def _(dve):
            n = [0]

            def link(ins):
                n[0] += 1
                ins.then_inc(s_dch, 1)
                dve.wait_ge(s_dch, n[0])

            full = [P, NB, D]

            def over_f(c):
                return c.unsqueeze(2).broadcast_to(full)

            def over_b(r):
                return r.unsqueeze(1).broadcast_to(full)

            dve.wait_ge(s_in, 16)
            dve.tensor_copy(bcast_src[0:1, 0:TR], cmp[0:1, 0:TR].bitcast(I32)).then_inc(s_dp, 1)
            dve.wait_ge(s_io, 10)
            dve.wait_ge(s_pp, 1)
            q = TR // 4
            for i in range(4):
                ins = dve.tensor_scalar(cmp[:, i * q:(i + 1) * q], PS[:, i, 0:q], col[:, 1:2], None, ALU.is_lt)
            link(ins)
            link(dve.reduce_sum(col[:, 2:3], cmp[:, 0:TR], axis=AX))
            link(dve.tensor_tensor(col[:, 2:3], col[:, 2:3], col[:, 0:1], ALU.add))
            dve.tensor_scalar(reach, reach, col[:, 2:3], None, ALU.is_gt).then_inc(s_dp, 1)
            dve.wait_ge(s_pp, 2)
            link(dve.tensor_copy(bcol[:, :], PS[:, 4, 0:SCH]))
            q = SW // 4
            for i in range(4):
                ins = dve.tensor_copy(brow[:, i * q:(i + 1) * q], PS[0:1, (5, 6, 7, 0)[i], 0:q])
            link(ins)
            link(dve.tensor_tensor(tcol[:, :], scol[:, :], bcol[:, :], ALU.subtract))
            dve.tensor_copy(ti[:, :], tcol[:, :]).then_inc(s_dp, 1)
            dve.wait_ge(s_io, 10)
            for i in range(4):
                link(dve.tensor_scalar(bcast_src[0:1, i * q:(i + 1) * q], PS[0:1, (5, 6, 7, 0)[i], 0:q], -1.0, None, ALU.mult))
            link(dve.tensor_tensor(bcast_src[0:1, 0:SW], bcast_src[0:1, 0:SW], srow[0:1, 0:SW], ALU.add))
            link(dve.tensor_copy(trow[:, :], bcast_src[0:1, 0:SW]))
            link(dve.tensor_copy(srow[0:1, 0:SW], brow[:, :]))
            link(dve.tensor_tensor(bcast_src[0:1, 1:SW], srow[0:1, 1:SW], srow[0:1, 0:SW - 1], ALU.not_equal))
            link(dve.tensor_scalar(bcast_src[0:1, 1:SW], bcast_src[0:1, 1:SW], BIG, None, ALU.mult))
            dve.memset(bcast_src[0:1, 0:1], BIG).then_inc(s_nb, 1)
            link(dve.tensor_scalar(bcol[:, :], bcol[:, :], float(P), None, ALU.mult))
            dve.wait_ge(s_er, 16 * 3 * SCH)
            for c in range(SCH):
                dve.tensor_copy(erow[0][:, c, :], erow[0][:, c, :].bitcast(I32))
                ins = dve.tensor_scalar(erow[1][:, c, :], erow[1][:, c, :].bitcast(I32), bcol[:, c:c + 1], None, ALU.subtract)
            ins.then_inc(s_dp, 1)
            for i in range(3 * SCH):
                dve.wait_ge(s_pp, 2 + i + 1)
                t = (idx, dstl, wst)[i % 3]
                dve.tensor_copy(t[:, i // 3 * P:(i // 3 + 1) * P], PS[:, i % 8, 0:P]).then_inc(s_dp, 1)
            dve.wait_ge(s_w, 16 * 18)
            dve.wait_ge(s_nbd, 16)
            dve.wait_ge(s_pp, 2 + 3 * SCH + 1)
            dve.memset(w4x[:, D:D + 1], 0.0)
            dve.tensor_copy(w4x[:, D + 1:D + 3], PS[0:D, 0, 0:2])
            dve.memset(col[:, 3:4], SOFT_EPS)
            link(dve.tensor_scalar(col[:, 4:5], col[:, 0:1], float(z.LAST), None, ALU.is_lt))

            def norm(v, a):
                link(dve.reduce_sum(st1[:, :], X[:, :, :], axis=AX))
                link(dve.tensor_scalar(st1[:, :], st1[:, :], 1.0 / D, None, ALU.mult))
                dve.tensor_tensor(H, X[:, :, :], over_f(st1[:, :]), ALU.subtract).then_inc(s_v2a, 1)
                dve.wait_ge(s_a2v, a)
                link(dve.reduce_sum(st2[:, :], A, axis=AX))
                dve.tensor_scalar(st2[:, :], st2[:, :], 1.0 / D, LN_EPS, ALU.mult, ALU.add).then_inc(s_v2a, 1)
                dve.wait_ge(s_a2v, a + 1)
                link(dve.reciprocal(st2[:, :], st2[:, :]))
                dve.tensor_tensor(H, H, over_f(st2[:, :]), ALU.mult).then_inc(s_v2a, 1)
                dve.wait_ge(s_a2v, a + 2)

            def dense(d):
                def turned_copy(g, i):
                    dve.wait_ge(d_tr, g * DU + (d * NB + i + 5))
                    w = 2 * P if d == 0 else P
                    dve.tensor_copy(tT[:, i % 4, 0:w], PS[0:D, i % 2, 0:w]).then_inc(d_tc, 1)

                def finish(g, i):
                    b = g * DU + i
                    if d == 1:
                        dve.wait_ge(d_m2, g * DU + (i + 1))
                        dve.tensor_copy(H[:, bass.DynSlice(b, 1), :].rearrange("p a f -> p (a f)"), PS[:, 4 + i % 4, 0:D]).then_inc(d_po, 1)
                        return
                    dve.wait_ge(d_m1, g * DU + (d * NB + i + 1))
                    if d == 3:
                        dve.tensor_copy(A3[:, bass.DynSlice(b, 1), :].rearrange("p a f -> p (a f)"), PS[:, 2 + i % 2, 0:D + 2])
                        dve.tensor_copy(adc[:, bass.DynSlice(b, 1)], PS[:, 2 + i % 2, D + 2:D + 3]).then_inc(d_po, 1)
                    else:
                        xb = X[:, bass.DynSlice(b, 1), :].rearrange("p a f -> p (a f)")
                        dve.tensor_tensor(xb, xb, PS[:, 2 + i % 2, 0:D], ALU.add).then_inc(d_po, 1)

                with dve.Fori(0, NB // DU) as g:
                    lagged(DU, (3 if d == 1 else 2, lambda i: finish(g, i)), (0, lambda i: turned_copy(g, i)))
                dve.wait_ge(d_po, (d + 1) * NB)

            regs = [dve.alloc_register(f"dve_block{k}") for k in range(RING)]

            def load_blocks(g, k, count=HALF):
                dve.load(regs[k:k + count], brow[0:1, bass.DynSlice(g * RING + k, count)])

            def steps(L):
                base, add_base = L * STEPS, L * (STEPS + 1) + 1
                acc, W = ((A, D), (A, D), (A2, 2 * D))[L]

                def one_hot(g, k):
                    s = g * RING + k
                    if L == 0:
                        dve.tensor_scalar(sel[:, k % 4, :], iota[:, :], dstl[:, bass.DynSlice(s, 1)], wst[:, bass.DynSlice(s, 1)],
                                          ALU.is_equal, ALU.mult).then_inc(sel_rdy, 1)
                    else:
                        dve.tensor_scalar(sel[:, k % 4, :], iota[:, :], dstl[:, bass.DynSlice(s, 1)], None,
                                          ALU.is_equal).then_inc(sel_rdy, 1)

                def pre_message(g, k):
                    dve.wait_ge(ea_mm, g * RING + (k + 1))
                    dve.wait_ge(gat[k], gat_val(L, g))
                    dve.tensor_tensor(pre[:, k % 4, 0:D], ering[:, k, 0:D], PS[:, 4 + k % 4, 0:D], ALU.add).then_inc(pre_rdy, 1)

                def add(g, k):
                    b = dve.snap(regs[k], min_val=0, max_val=NB - 1)
                    ab = acc[:, bass.DynSlice(b, 1), :].rearrange("p a f -> p (a f)")
                    dve.wait_ge(slot_free, g * RING + (base + RING + k + 1))
                    dve.wait_ge(added, g * RING + (add_base + k))
                    dve.tensor_tensor(ab, ab, PS[:, k % 4, 0:W], ALU.add).then_inc(added, 1)

                dve.memset(acc, 0.0).then_inc(added, 1)
                if L == 1:
                    pipelined(dve, (0, one_hot), (0, pre_message), (3, add), load=load_blocks)
                else:
                    pipelined(dve, (0, one_hot), (2, add), load=load_blocks)
                dve.wait_ge(added, add_base + STEPS)

            norm(0, 1)
            dve.sem_inc(tab_ready[0], 1)
            steps(0)
            dense(0)
            link(dve.memset(eatt[DE:DE + 1, :, :], 1.0))
            norm(3, 4)
            dve.sem_inc(tab_ready[1], 1)
            steps(1)
            dve.tensor_tensor(H, H, A, ALU.add).then_inc(s_v2a, 1)
            dense(1)
            link(dve.tensor_scalar(H[:, NB - 1, :], H[:, NB - 1, :], col[:, 4:5], None, ALU.mult))
            dve.reduce_sum(bs[:, 0, :], H.rearrange("p b f -> p f b"), axis=AX).then_inc(s_bnp, 1)
            dve.wait_ge(s_bnp, 2)
            link(dve.tensor_scalar(bs[:, 2, :], PS[:, 0, 0:D], 1.0 / z.N, None, ALU.mult))
            link(dve.tensor_tensor(H, H, over_b(bs[:, 2, :]), ALU.subtract))
            dve.tensor_scalar(H[:, NB - 1, :], H[:, NB - 1, :], col[:, 4:5], None, ALU.mult).then_inc(s_v2a, 1)
            dve.wait_ge(s_a2v, 7)
            dve.reduce_sum(bs[:, 1, :], A.rearrange("p b f -> p f b"), axis=AX).then_inc(s_bnp, 1)
            dve.wait_ge(s_bnp, 4)
            dve.tensor_scalar(bs[:, 1, :], PS[:, 1, 0:D], 1.0 / z.N, BN_EPS, ALU.mult, ALU.add).then_inc(s_v2a, 1)
            dve.wait_ge(s_a2v, 8)
            link(dve.reciprocal(bs[:, 1, :], bs[:, 1, :]))
            link(dve.tensor_tensor(bs[:, 1, :], bs[:, 1, :], bn[:, 0, :], ALU.mult))
            link(dve.tensor_tensor(H, H, over_b(bs[:, 1, :]), ALU.mult))
            dve.tensor_tensor(H, H, over_b(bn[:, 1, :]), ALU.add).then_inc(s_v2a, 1)
            dve.wait_ge(s_a2v, 9)
            link(dve.tensor_tensor(X[:, :, :], X[:, :, :], H, ALU.add))
            norm(11, 10)
            link(dve.tensor_scalar(A2[:, :, D:2 * D], H, SOFT_EPS, None, ALU.add))
            link(dve.tensor_tensor(A2[:, :, D:2 * D], A2[:, :, D:2 * D], A2[:, :, 0:D], ALU.mult))
            dve.sem_inc(tab_ready[2], 1)
            dve.wait_ge(tab_wr[2], 16)
            steps(2)
            link(dve.tensor_scalar(A2[:, :, 0:D], A2[:, :, 0:D], 1.0, None, ALU.max))
            link(dve.reciprocal(A2[:, :, 0:D], A2[:, :, 0:D]))
            link(dve.tensor_tensor(A2[:, :, 0:D], A2[:, :, 0:D], A2[:, :, D:2 * D], ALU.mult))
            dve.tensor_tensor(H, H, A2[:, :, 0:D], ALU.add).then_inc(s_v2a, 1)
            dense(2)
            norm(15, 13)
            dense(3)
            add_base = 3 * (STEPS + 1) + 1
            dve.memset(A3[:, :, D:D + 1], 1.0).then_inc(added, 1)
            dve.wait_ge(added, add_base)
            dve.sem_inc(tab_ready[3], 1)
            dve.tensor_tensor(lc[:, :], A3[:, :, D + 1:D + 2].rearrange("p b a -> p (b a)"), adc[:, :], ALU.add).then_inc(s_v2a, 1)
            dve.wait_ge(s_v2a, 18)
            link(dve.scalar_tensor_tensor(out=lc[:, :], in0=lc[:, :], scalar=SLOPE, in1=lc[:, :], op0=ALU.mult, op1=ALU.max))
            link(dve.tensor_scalar(lc[:, :], lc[:, :], -1.0, None, ALU.mult))
            dve.tensor_scalar(dstl[:, :], dstl[:, :], -BIG, None, ALU.mult).then_inc(s_v2a, 1)
            dve.wait_ge(s_adT, 1)
            dve.tensor_copy(adT[:, :], PS[0:NB, 6, 0:P]).then_inc(s_adS, 1)
            dve.wait_ge(tab_wr[3], 16)
            dve.wait_ge(s_adR, 16)

            base = 3 * STEPS

            def next_blocks(g, k):
                if k % 4 == 0:
                    load_blocks(g, k, 4)

            def raw_logits(g, k):
                b = dve.snap(regs[k], min_val=0, max_val=NB - 1)
                dve.wait_ge(z_rdy, g * RING + (k + 1))
                dve.scalar_tensor_tensor(out=raw[:, k % 4, :], in0=zb[:, k % 8, :], scalar=ering[:, k, D + 1:D + 2],
                                         in1=adrow[:, bass.DynSlice(b * P, P)], op0=ALU.subtract, op1=ALU.subtract)\
                    .then_inc(raw_rdy, 1)

            def leaky(g, k):
                dve.wait_ge(raw_rdy, g * RING + (k + 1))
                dve.wait_ge(prd, g * RING + (k + 1))
                z = raw[:, k % 4 - 1:k % 4 + 1, :]
                dve.scalar_tensor_tensor(out=logit[:, k % 8 - 1:k % 8 + 1, :], in0=z, scalar=SLOPE, in1=z,
                                         op0=ALU.mult, op1=ALU.min).then_inc(u_rdy, 2)

            def tile_max(g, k):
                dve.wait_ge(psa, g * RING + (k + 1))
                dve.tensor_reduce(cm[:, k - 1:k + 1], PS[:, k // 2 % 2, 0:2 * P].rearrange("p (s e) -> p s e", s=2), AX, ALU.min)\
                    .then_inc(cmx, 2)

            def old_max(g, k):
                b = dve.snap(regs[k], min_val=0, max_val=NB - 1)
                before = ln_[:, (k - 1) % RING:(k - 1) % RING + 1]
                dve.wait_ge(lcn, g * RING + (k + 1))
                dve.scalar_tensor_tensor(out=old[:, k:k + 1], in0=before, scalar=wst[:, bass.DynSlice(g * RING + k, 1)],
                                         in1=lc[:, bass.DynSlice(b, 1)], op0=ALU.add, op1=ALU.min).then_inc(oldr, 1)

            def new_max(g, k):
                dve.wait_ge(oldr if k % 2 else cmx, g * RING + (k + 1))
                dve.tensor_tensor(ln_[:, k:k + 1], cm[:, k:k + 1], old[:, k:k + 1], ALU.min).then_inc(lcn, 1)

            def shifted(g, k):
                dve.wait_ge(psc, g * RING + (k + 1))
                z = logit[:, k % 8 - 1:k % 8 + 1, :]
                dve.tensor_tensor(z, z, PS[:, 2 + k // 2 % 2, 0:2 * P].rearrange("p (s e) -> p s e", s=2), ALU.subtract)\
                    .then_inc(xrd, 2)

            def add_scaled(g, k):
                b = dve.snap(regs[k], min_val=0, max_val=NB - 1)
                ab = A3[:, bass.DynSlice(b, 1), 0:D + 1].rearrange("p a f -> p (a f)")
                if isinstance(g, int):
                    dve.wait_ge(added, g * RING + (add_base + k))
                dve.wait_ge(slot_free, g * RING + (base + RING + k + 1))
                dve.scalar_tensor_tensor(out=ab, in0=ab, scalar=fac[:, k:k + 1], in1=PS[:, 4 + k % 4, 0:D + 1],
                                         op0=ALU.mult, op1=ALU.add).then_inc(added, 1)

            dve.memset(ln_[:, RING - 1:RING], 0.0).then_inc(lcn, 1)
            dve.wait_ge(s_nbl, 16)
            pipelined(dve, (12, add_scaled), (8, shifted, "pair"), (1, next_blocks), (6, old_max), (5, tile_max, "pair"), (2, raw_logits),
                      (3, leaky, "pair"), (6, new_max))
            dve.wait_ge(added, add_base + STEPS)
            den = A3[:, :, D:D + 1].rearrange("p b a -> p (b a)")
            link(dve.tensor_scalar(st1[:, :], den, GAT_EPS, None, ALU.add))
            link(dve.reciprocal(st1[:, :], st1[:, :]))
            link(dve.tensor_tensor(H, A3[:, :, 0:D], over_f(st1[:, :]), ALU.mult))
            dve.tensor_tensor(H, H, over_b(bn[:, 2, :]), ALU.add).then_inc(s_v2a, 1)
            dve.wait_ge(s_a2v, 16)
            dve.tensor_tensor(X[:, :, :], X[:, :, :], A, ALU.add).then_inc(s_fin, 1)


def kernel(x, src, dst, edge_attr_32, edge_weight, L0_gnn_mlp_w, L0_gnn_mlp_b, L1_gnn_We, L1_gnn_be, L1_gnn_W1,
           L1_gnn_b1, L1_gnn_W2, L1_gnn_b2, L1_gnn_gamma, L1_gnn_beta, L2_gnn_W, L2_gnn_b, L3_gnn_W,
           L3_gnn_att_src, L3_gnn_att_dst, L3_gnn_bias):
    import concourse.bacc as bacc
    from concourse.bass_utils import run_bass_kernel_spmd as run

    z = Sizes(x.shape[0], src.shape[0])

    def rows(a, fill):
        a = np.asarray(a)
        full = np.full((z.TR * P,) + a.shape[1:], fill, a.dtype)
        full[:a.shape[0]] = a
        return full.reshape((z.TR, P) + a.shape[1:])

    arrays = {
        "x": np.asarray(x), "src": rows(src, 0), "dst": rows(dst, NO_NODE), "ew": rows(edge_weight, 0),
        "eaT": rows(edge_attr_32, 0).transpose(0, 2, 1),
        "w0T": np.asarray(L0_gnn_mlp_w).T, "b0": L0_gnn_mlp_b, "We": L1_gnn_We, "be": L1_gnn_be, "W1": L1_gnn_W1,
        "b1": L1_gnn_b1, "W2": L1_gnn_W2, "b2": L1_gnn_b2, "gamma": L1_gnn_gamma, "beta": L1_gnn_beta,
        "W3": L2_gnn_W, "b3": L2_gnn_b, "W4": L3_gnn_W, "W4T": np.asarray(L3_gnn_W).T,
        "att": np.stack([np.asarray(L3_gnn_att_src), np.asarray(L3_gnn_att_dst)], axis=1), "bias4": L3_gnn_bias,
    }
    arrays = {k: np.ascontiguousarray(a) for k, a in arrays.items()}
    nc = bacc.Bacc("TRN2", target_bir_lowering=False, num_devices=1)
    aps = {k: nc.dram_tensor(f"in_{k}", a.shape, mybir.dt.from_np(a.dtype), kind="ExternalInput").ap()
           for k, a in arrays.items()}
    out = nc.dram_tensor("out_0", tuple(x.shape), F32, kind="ExternalOutput").ap()
    build(nc, z, out=out, **aps)
    r = run(nc, [{f"in_{k}": a for k, a in arrays.items()}], core_ids=[0])
    return r.results[0]["out_0"]
```

```python
from contextlib import ExitStack

import numpy as np

import concourse.bass as bass
from concourse import mybir

F32 = mybir.dt.float32
BF16 = mybir.dt.bfloat16
I32 = mybir.dt.int32
ALU = mybir.AluOpType
ACT = mybir.ActivationFunctionType
AX = mybir.AxisListType.X
P = 128
D = 96
DE = 32
RING = 16
HALF = RING // 2
NO_NODE = 1 << 20
BIG = 2.0 ** 100
LN_EPS = 1e-5
BN_EPS = 1e-5
SOFT_EPS = 1e-7
NO_EDGE = 1e-30
GAT_EPS = 1e-16
SLOPE = 0.2


class Sizes:
    def __init__(self, nodes, edges):
        self.N, self.E = nodes, edges
        self.NB = -(-nodes // P)
        self.NB += self.NB % 2
        self.LAST = nodes - (self.NB - 1) * P
        self.TILES = -(-edges // P)
        self.ITERS = -(-(self.TILES + self.NB - 1) // RING)
        self.STEPS = self.ITERS * RING
        self.SCH = -(-self.STEPS // P)
        self.SW = self.SCH * P
        rows = max(self.TILES, self.SW - self.NB + 1)
        self.TR = rows + (-rows) % 4
        self.DU = max(u for u in range(2, 17, 2) if self.NB % u == 0)
        self.CH = self.NB // self.DU
        assert self.LAST > 0 and D * self.NB >= RING * P + self.SW and 2 * D * self.NB >= self.TR + 7 * self.SW and self.STEPS % 4 == 0 and self.STEPS // 4 <= 512 and self.TR // 4 <= 512


def build(nc, z, x, src, dst, ew, eaT, w0T, b0, We, be, W1, b1, W2, b2, gamma, beta, W3, b3, W4, W4T, att, bias4, out):
    NB, SCH, SW, STEPS, ITERS, TR, DU, CH = z.NB, z.SCH, z.SW, z.STEPS, z.ITERS, z.TR, z.DU, z.CH
    ctx = ExitStack()
    with ctx:
        def sb(name, shape, dt=F32):
            return ctx.enter_context(nc.sbuf_tensor(name, shape, dt))

        def sem(name):
            return ctx.enter_context(nc.semaphore(name))

        tab = [nc.dram_tensor(f"table{i}", (NB * P, w), F32).ap() for i, w in enumerate((D, D, 2 * D, D + 2))]
        new_dram = nc.dram_tensor("new_block_dram", (1, SW), F32).ap()
        ad_dram = nc.dram_tensor("ad_dram", (NB, P), F32).ap()

        X = sb("X", [P, NB, D])
        R = sb("R", [P, NB * 3 * D])
        H = R[:, 2 * D * NB:3 * D * NB].rearrange("p (b f) -> p b f", f=D)
        A = R[:, 0:D * NB].rearrange("p (b f) -> p b f", f=D)
        A2 = R[:, 0:2 * D * NB].rearrange("p (b f) -> p b f", f=2 * D)
        A3 = R[:, 0:(D + 2) * NB].rearrange("p (b f) -> p b f", f=D + 2)
        adrow = R[:, (D + 2) * NB:(D + 2 + P) * NB]
        cmp = R[:, 0:TR]
        reach = R[:, TR:TR + SW]
        srow = R[:, TR + 4 * SW:TR + 5 * SW]
        bcast_src = R[:, TR + 5 * SW:TR + 5 * SW + max(TR, SW)]
        erow = [R[:, TR + SW + i * SW:TR + SW + (i + 1) * SW].rearrange("p (c e) -> p c e", e=P) for i in range(3)]
        ering = sb("gathered_rows", [P, RING, 2 * D])
        work = sb("work", [P, 8 * D + 12 * P])
        raw, msg, pre, sel = (work[:, i * 4 * P:(i + 1) * 4 * P].rearrange("p (r e) -> p r e", r=4) for i in range(4))
        logit = work[:, 4 * P:12 * P].rearrange("p (r e) -> p r e", r=8)
        stg = work[:, 0:8 * D].rearrange("p (r f) -> p r f", r=4)
        tT = work[0:D + 1, 8 * D:8 * D + 8 * P].rearrange("p (r n) -> p r n", r=4)
        rT = work[0:D + 1, 8 * D + 8 * P:8 * D + 12 * P].rearrange("p (r n) -> p r n", r=4)
        ones_rows = work[D:D + 1, 8 * D:8 * D + 12 * P]
        zb = sb("off_block", [P, 8, P], BF16)
        eatt = R[0:DE + 1, D * NB:D * NB + RING * P].rearrange("p (k e) -> p k e", k=RING)
        ib = sb("staged_index", [P, RING], I32)
        idx = sb("src_of_step", [P, SW], I32)
        dstl = sb("dst_in_block", [P, SW])
        wst = sb("weight_of_step", [P, SW])
        brow = sb("block_of_step", [1, SW], I32)
        trow = R[0:1, 2 * D * NB - SW:2 * D * NB].bitcast(I32)
        iota = sb("iota", [P, P])
        ident = sb("ident", [P, P])
        ones = sb("ones", [P, P])
        col = sb("cols", [P, 16])
        scol = sb("step_col", [P, SCH])
        bcol = sb("block_col", [P, SCH])
        tcol = sb("tile_col", [P, SCH])
        ti = sb("tile_idx", [P, SCH], I32)
        st1 = sb("ln_mean", [P, NB])
        st2 = sb("ln_rstd", [P, NB])
        w0 = sb("w0", [D + 1, 2, D])
        wew = sb("we", [DE + 1, D])
        w1 = sb("w1", [D, D])
        w2 = sb("w2", [D + 1, D])
        w3 = sb("w3", [D + 1, D])
        w4x = sb("w4x", [D + 1, D + 3])
        w4t = sb("w4t", [D, D])
        att2 = sb("att2", [D, 2])
        b1c = sb("b1c", [D, 1])
        bn = sb("bn_rows", [P, 3, D])
        bs = sb("bn_stats", [P, 3, D])
        adc = sb("ad_col", [P, NB])
        adT = sb("ad_T", [NB, P])
        lc = sb("run_max", [P, NB])
        cm = sb("tile_max", [P, RING])
        ln_ = sb("new_max", [P, RING])
        old = sb("old_max", [P, RING])
        fac = sb("rescale", [P, RING])
        PS = ctx.enter_context(nc.psum_tensor("PS", [P, 8, 512], F32))

        s_in = sem("inputs_loaded")
        s_w = sem("weights_loaded")
        s_io = sem("pool_consts")
        s_dp = sem("dve_prep")
        s_pp = sem("pe_prep")
        s_er = sem("edge_rows_gathered")
        s_dch = sem("dve_chain")
        s_ach = sem("act_chain")
        s_v2a = sem("dve_to_act")
        s_a2v = sem("act_to_dve")
        ln_sum, ln_mean, ln_cen, ln_ssq, ln_var, ln_inv, ln_scl = (
            sem(f"norm_{n}") for n in ("sum", "mean", "centred", "square_sum", "variance", "inverse", "scaled"))
        ln_sq, ln_dev = sem("norm_squares"), sem("norm_deviation")
        bn_cen, bn_sq, bn_aff, bn_rel = (sem(f"batchnorm_{n}") for n in ("centred", "squares", "scaled", "relu"))
        dv_inv, dv_div = sem("layer2_inverse_ready"), sem("layer2_input_ready")
        h_sum, message = sem("layer1_sum_ready"), sem("layer2_message_ready")
        h_new = sem("relu_ready")
        s_bnp = sem("bn_summed")
        tab_ready = [sem(f"table_values{i}") for i in range(3)]
        tab_wr = [sem(f"table_written{i}") for i in range(4)]
        staged = [sem(f"index_staged{h}") for h in range(2)]
        gat = [sem(f"gathered{k}") for k in range(RING)]
        eah = [sem(f"edge_features_loaded{k}") for k in range(RING)]
        ea_ones = sem("edge_bias_row_ready")
        slot_free = sem("slot_free")
        sel_rdy = sem("one_hot_ready")
        added = sem("block_added")
        ea_mm = sem("edge_product_ready")
        pre_rdy = sem("pre_message_ready")
        msg_rdy = sem("message_ready")
        raw_rdy = sem("raw_logits_ready")
        u_rdy = sem("logits_ready")
        oldr = sem("old_max_ready")
        z_rdy = sem("off_block_ready")
        psa = sem("logits_turned")
        cmx = sem("tile_max_ready")
        s_nb = sem("new_block_row_ready")
        s_nbd = sem("new_block_row_in_dram")
        s_nbl = sem("new_block_rows_loaded")
        lcn = sem("new_max_ready")
        psc = sem("max_rows_ready")
        xrd = sem("shifted_ready")
        prd = sem("weights_ready")
        d_st = sem("dense_staged")
        d_tr = sem("dense_turned")
        d_tc = sem("dense_turned_copied")
        d_m1 = sem("dense_product1")
        d_re = sem("dense_relu")
        d_m2 = sem("dense_product2")
        d_po = sem("dense_done")
        s_adT = sem("ad_turned")
        s_adS = sem("ad_copied")
        s_adD = sem("ad_in_dram")
        s_adR = sem("ad_rows_loaded")
        out_in, out_tanh = sem("tanh_input_ready"), sem("tanh_ready")
        s_fin = sem("result_ready")
        s_out = sem("result_stored")

        block = ctx.enter_context(nc.Block())

        def gat_val(L, g):
            return g * 16 + (16 * (L * ITERS) + 16)

        def half_bank(bank, k):
            return PS[:, bank + k // 2 % 2, k % 2 * P:(k % 2 + 1) * P]

        def lagged(n, *stages, extra={}):
            top = max(l for l, _ in stages)
            for i in range(n + top):
                if i in extra:
                    extra[i]()
                for lag, fn in stages:
                    if 0 <= i - lag < n:
                        fn(i - lag)

        def squares(n, c):
            if n > 0:
                return A[:, cut(c), :]
            flat = ering[:, :, :].rearrange("p r f -> p (r f)")
            return flat[:, c % 2 * DU * D:(c % 2 + 1) * DU * D].rearrange("p (b f) -> p b f", f=D)

        def cut(c):
            return bass.DynSlice(c * DU, DU)

        def chunk_loop(eng, blocks, after=()):
            def extras(g):
                return {p: (lambda fn=fn: fn(g - 1)) for p, fn in after}

            if not after:
                with eng.Fori(0, CH) as g:
                    blocks(g, {})
                return
            blocks(0, {})
            if CH > 2:
                with eng.Fori(1, CH - 1) as g:
                    blocks(g, extras(g))
            if CH > 1:
                blocks(CH - 1, extras(CH - 1))
            for p, fn in after:
                fn(CH - 1)

        def pipelined(eng, *stages, load=None):
            top = max(s[0] for s in stages)
            earliest = min(s[0] for s in stages)

            def issue(g, first, limit):
                for lag, fn, *pair in stages:
                    c = first - lag
                    if 0 <= c < limit and (not pair or c % 2 == 1):
                        if lag == earliest and load is not None and c % HALF == 0:
                            load(g + c // RING, c % RING)
                        fn(g + c // RING, c % RING)

            for i in range(top):
                issue(0, i, STEPS)
            with eng.Fori(0, ITERS - 1) as g:
                for j in range(RING):
                    issue(g, top + j, STEPS)
            for j in range(RING):
                issue(ITERS - 1, top + j, RING)

        @block.sync
        def _(sp):
            with nc.allow_non_contiguous_dma(reason="one destination per tile"):
                sp.dma_start(cmp[0:1, 0:TR].bitcast(I32), dst[:, P - 1:P].rearrange("t a -> a t")).then_inc(s_in, 16)
            sp.wait_ge(s_io, 1)
            sp.dma_start(X[:, 0:NB - 1, :], x[0:(NB - 1) * P, :].rearrange("(b p) f -> p b f", p=P)).then_inc(s_w, 16)
            sp.dma_start(X[0:z.LAST, NB - 1, :], x[(NB - 1) * P:z.N, :]).then_inc(s_w, 16)
            sp.dma_start(w0[0:D, :, :], w0T.rearrange("(h i) o -> i h o", h=2)).then_inc(s_w, 16)
            sp.dma_start(wew[0:DE, :], We).then_inc(s_w, 16)
            sp.dma_start(wew[DE:DE + 1, :], be.rearrange("(a n) -> a n", a=1)).then_inc(s_w, 16)
            for t, s in ((w1, W1), (w2, W2), (w3, W3), (w4t, W4T)):
                sp.dma_start(t[0:D, :], s).then_inc(s_w, 16)
            sp.dma_start(w4x[0:D, 0:D], W4).then_inc(s_w, 16)
            sp.dma_start(att2[:, :], att).then_inc(s_w, 16)
            sp.dma_start(b1c[:, :], b1.rearrange("(n a) -> n a", a=1)).then_inc(s_w, 16)
            for t, s in ((w0[D:D + 1, 1, :], b0), (w2[D:D + 1, :], b2), (w3[D:D + 1, :], b3)):
                sp.dma_start(t, s.rearrange("(a n) -> a n", a=1)).then_inc(s_w, 16)
            for i, s in enumerate((gamma, beta, bias4)):
                sp.dma_start(bn[:, i, :], s.rearrange("(a n) -> a n", a=1).broadcast_to([P, D])).then_inc(s_w, 16)

            sp.wait_ge(s_nb, 1)
            sp.dma_start(new_dram, bcast_src[0:1, 0:SW]).then_inc(s_nbd, 16)
            sp.wait_ge(s_nbd, 16)
            def stage_indices(L, g):
                for h in range(2):
                    if L > 0 or not isinstance(g, int):
                        for k in range(h * HALF, (h + 1) * HALF):
                            sp.wait_ge(gat[k], g * 16 + 16 * L * ITERS)
                    sp.dma_start(ib[:, h * HALF:(h + 1) * HALF], idx[:, bass.DynSlice(g * RING + h * HALF, HALF)])\
                        .then_inc(staged[h], 16)

            for L in range(4):
                if L > 0:
                    stage_indices(L, 0)
                vals = (H, H, A2, A3)[L]
                for c in range(CH):
                    if L < 3:
                        sp.wait_ge(tab_ready[L], c + 1)
                    else:
                        sp.wait_ge(d_po, 3 * NB + (c + 1) * DU)
                    sp.dma_start(tab[L].rearrange("(b p) f -> p b f", p=P)[:, c * DU:(c + 1) * DU, :], vals[:, c * DU:(c + 1) * DU, :])\
                        .then_inc(tab_wr[L], 16)
                if L == 1:
                    sp.dma_start(wst[:, :], new_dram.broadcast_to([P, SW])).then_inc(s_nbl, 16)
                if L == 3:
                    sp.wait_ge(s_adS, 1)
                    sp.dma_start(ad_dram, adT[:, :]).then_inc(s_adD, 16)
                    sp.wait_ge(s_adD, 16)
                    sp.dma_start(adrow, ad_dram.rearrange("(a b) p -> a (b p)", a=1).broadcast_to([P, NB * P]))\
                        .then_inc(s_adR, 16)
                if L == 0:
                    sp.wait_ge(s_dp, 4 + 3 * SCH)
                    stage_indices(0, 0)
                with sp.Fori(1, ITERS) as g:
                    stage_indices(L, g)
            for c in range(CH):
                sp.wait_ge(s_fin, c + 1)
                a, b = c * DU, min((c + 1) * DU, NB - 1)
                sp.dma_start(out[a * P:b * P, :].rearrange("(b p) f -> p b f", p=P), X[:, a:b, :]).then_inc(s_out, 16)
            sp.dma_start(out[(NB - 1) * P:z.N, :], X[0:z.LAST, NB - 1, :]).then_inc(s_out, 16)
            sp.wait_ge(s_out, 16 * (CH + 1))

        @block.gpsimd
        def _(pool):
            pool.memset(X[:, NB - 1, :], 0.0).then_inc(s_io, 1)
            pool.iota(iota[:, :], pattern=[[1, P]], base=0, channel_multiplier=0, allow_small_or_imprecise_dtypes=True).then_inc(s_io, 1)
            pool.iota(reach, pattern=[[1, SW]], base=0, channel_multiplier=0, allow_small_or_imprecise_dtypes=True).then_inc(s_io, 1)
            pool.iota(srow[0:1, :], pattern=[[1, SW]], base=0, channel_multiplier=0, allow_small_or_imprecise_dtypes=True).then_inc(s_io, 1)
            pool.iota(scol[:, :], pattern=[[P, SCH]], base=0, channel_multiplier=1, allow_small_or_imprecise_dtypes=True).then_inc(s_io, 1)
            pool.iota(col[:, 0:1], pattern=[[0, 1]], base=0, channel_multiplier=1, allow_small_or_imprecise_dtypes=True).then_inc(s_io, 1)
            pool.iota(col[:, 1:2], pattern=[[0, 1]], base=P, channel_multiplier=P, allow_small_or_imprecise_dtypes=True).then_inc(s_io, 1)
            pool.memset(ones[:, :], 1.0).then_inc(s_io, 1)
            pool.memset(ident[:, :], 0.0).then_inc(s_io, 1)
            pool.wait_ge(s_io, 9)
            pool.affine_select(out=ident[:, :], in_=ident[:, :], compare_op=ALU.not_equal, fill=1.0, base=0,
                               pattern=[[-1, P]], channel_multiplier=1).then_inc(s_io, 1)
            pool.wait_ge(s_dp, 3)
            for c in range(SCH):
                for r, t in zip(erow, (src, dst, ew)):
                    o = r[:, c, :] if t is ew else r[:, c, :].bitcast(I32)
                    pool.indirect_dma_start(o, None, t, bass.IndirectOffsetOnAxis(ap=ti[:, c:c + 1], axis=0))\
                        .then_inc(s_er, 16)
            for L in range(4):
                W = (D, D, 2 * D, D + 2)[L]
                few = (4, 4, 4, 2)[L]
                if L == 2:
                    pool.wait_ge(added, 2 * (STEPS + 1))
                    for c in range(CH):
                        pool.tensor_tensor(H[:, cut(c), :], H[:, cut(c), :], A[:, cut(c), :], ALU.add).then_inc(h_sum, 1)
                if L == 3:
                    for c in range(CH):
                        e, m = A2[:, cut(c), 0:D], A2[:, cut(c), D:2 * D]
                        pool.wait_ge(dv_inv, (c + 1) * DU)
                        pool.tensor_tensor(e, e, m, ALU.mult).then_inc(message, 1)
                        pool.wait_ge(message, c + 1)
                        pool.tensor_tensor(H[:, cut(c), :], H[:, cut(c), :], e, ALU.add).then_inc(dv_div, 1)
                pool.wait_ge(tab_wr[L], 16 * CH)
                with pool.Fori(0, ITERS) as g:
                    for h in range(2):
                        pool.wait_ge(staged[h], g * 16 + (16 * (L * ITERS) + 16))
                        pool.nop(nofuse=True)
                        for k in range(h * HALF, (h + 1) * HALF):
                            if k % few == 0:
                                pool.wait_ge(slot_free, g * RING + (L * STEPS + k + few))
                                pool.nop(nofuse=True)
                            pool.indirect_dma_start(ering[:, k, 0:W], None, tab[L],
                                                    bass.IndirectOffsetOnAxis(ap=ib[:, k:k + 1], axis=0)).then_inc(gat[k], 16)

        @block.tensor
        def _(pe):
            pe.sem_inc(slot_free, RING)
            pe.sem_inc(d_tr, 4)
            pe.sem_inc(prd, 8)
            pe.wait_ge(s_io, 10)
            pe.wait_ge(s_dp, 1)
            q = TR // 4
            for i in range(4):
                last = pe.matmul(PS[:, i, 0:q], ones[0:1, :], bcast_src[0:1, i * q:(i + 1) * q], start=True, stop=True)
            last.then_inc(s_pp, 1)
            pe.wait_ge(s_dp, 2)
            for c in range(SCH):
                pe.matmul(PS[:, 4, c:c + 1], reach[0:NB - 1, c * P:(c + 1) * P], ones[0:NB - 1, 0:1], start=True, stop=True)
            q = SW // 4
            for i in range(4):
                last = pe.matmul(PS[0:1, (5, 6, 7, 0)[i], 0:q], ones[0:NB - 1, 0:1], reach[0:NB - 1, i * q:(i + 1) * q],
                                 start=True, stop=True)
            last.then_inc(s_pp, 1)
            pe.wait_ge(s_dp, 4)
            for i in range(3 * SCH):
                if i >= 8:
                    pe.wait_ge(s_dp, 4 + i - 7)
                pe.transpose(PS[:, i % 8, 0:P], erow[i % 3][:, i // 3, :], ident[:, :]).then_inc(s_pp, 1)
            pe.wait_ge(s_w, 16 * 18)
            pe.wait_ge(s_dp, 4 + 3 * SCH)
            pe.matmul(PS[0:D, 0, 0:2], w4t[:, :], att2[:, :], start=True, stop=True).then_inc(s_pp, 1)
            base_pp = 2 + 3 * SCH + 1

            def dense(d):
                halves = 2 if d == 0 else 1

                def turn(g, i):
                    pe.wait_ge(d_st, g * DU + (d * NB + i + 1))
                    for q in range(halves):
                        last = pe.transpose(PS[0:D, i % 2, q * P:(q + 1) * P], stg[:, i % 4, q * D:(q + 1) * D], ident[:, :])
                    last.then_inc(d_tr, 1)

                def product1(g, i):
                    pe.wait_ge(d_tc, g * DU + (d * NB + i + 1))
                    o = PS[:, 2 + i % 4, 0:(D + 3 if d == 3 else D)]
                    t = tT[:, i % 4, :]
                    if d == 0:
                        pe.matmul(o, t[0:D, 0:P], w0[0:D, 0, :], start=True, stop=False)
                        pe.matmul(o, t[:, P:2 * P], w0[:, 1, :], start=False, stop=True).then_inc(d_m1, 1)
                    elif d == 1:
                        pe.matmul(PS[0:D, 2 + i % 2, 0:P], w1[:, :], t[0:D, 0:P], start=True, stop=True).then_inc(d_m1, 1)
                    elif d == 2:
                        pe.matmul(o, t[:, 0:P], w3[:, :], start=True, stop=True).then_inc(d_m1, 1)
                    else:
                        pe.matmul(o, t[:, 0:P], w4x[:, :], start=True, stop=True).then_inc(d_m1, 1)

                def product2(g, i):
                    pe.wait_ge(d_re, g * DU + (i + 1))
                    o = PS[:, 4 + i % 4, 0:D]
                    pe.matmul(o, rT[:, i % 4, :], w2[:, :], start=True, stop=True).then_inc(d_m2, 1)

                with pe.Fori(0, NB // DU) as g:
                    stages = [(0, lambda i: turn(g, i)), (1, lambda i: product1(g, i))]
                    if d == 1:
                        stages.append((2, lambda i: product2(g, i)))
                    lagged(DU, *stages)

            def steps(L):
                base = L * STEPS
                W = (D, D, 2 * D)[L]

                def edge_product(g, k):
                    pe.wait_ge(eah[k], g * 16 + 16)
                    pe.matmul(PS[:, 4 + k % 4, 0:D], eatt[:, k, :], wew[:, :], start=True, stop=True).then_inc(ea_mm, 1)

                def sum_tile(g, k):
                    pe.wait_ge(sel_rdy, g * RING + (base + k + 1))
                    if L == 1:
                        pe.wait_ge(msg_rdy, g * RING + (k + 1))
                        rhs = msg[:, k % 4, 0:D]
                    else:
                        pe.wait_ge(gat[k], gat_val(L, g))
                        rhs = ering[:, k, 0:W]
                    pe.matmul(PS[:, k % 4, 0:W], sel[:, k % 4, :], rhs, start=True, stop=True).then_inc(slot_free, 1)

                if L == 1:
                    pe.wait_ge(ea_ones, 1)
                    pipelined(pe, (0, edge_product), (2, sum_tile))
                else:
                    pipelined(pe, (0, sum_tile))

            def attention_steps():
                def turn_logits(g, k):
                    pe.wait_ge(u_rdy, g * RING + (k + 1))
                    for j in (k - 1, k):
                        pe.transpose(half_bank(0, j), logit[:, j % 8, :], ident[:, :]).then_inc(psa, 1)

                def spread_max(g, k):
                    pe.wait_ge(lcn, g * RING + (k + 2))
                    for j in (k - 1, k):
                        pe.transpose(half_bank(2, j), ln_[:, j:j + 1].broadcast_to([P, P]), ident[:, :]).then_inc(psc, 1)

                def sum_tile(g, k):
                    pe.wait_ge(prd, g * RING + (k + 9))
                    pe.wait_ge(gat[k], gat_val(3, g))
                    pe.matmul(PS[:, 4 + k % 4, 0:D + 1], sel[:, k % 4, :], ering[:, k, 0:D + 1], start=True, stop=True)\
                        .then_inc(slot_free, 1)

                pipelined(pe, (10, sum_tile), (3, turn_logits, "pair"), (6, spread_max, "pair"))

            steps(0)
            dense(0)
            steps(1)
            dense(1)
            for i in range(2):
                pe.wait_ge(s_bnp, 2 * i + 1)
                pe.matmul(PS[:, i, 0:D], ones[:, :], bs[:, i, :], start=True, stop=True).then_inc(s_bnp, 1)
            steps(2)
            dense(2)
            dense(3)
            pe.wait_ge(d_po, 4 * NB)
            pe.transpose(PS[0:NB, 6, 0:P], adc[:, :], ident[:, :]).then_inc(s_adT, 1)
            attention_steps()

        @block.scalar
        def _(act):
            n = [0]

            def link(ins):
                n[0] += 1
                ins.then_inc(s_ach, 1)
                act.wait_ge(s_ach, n[0])

            def square(n, c):
                act.wait_ge(ln_cen, c + (n * CH + 1))
                if n == 0 and c >= 2:
                    act.wait_ge(ln_ssq, c - 1)
                act.nop(nofuse=True)
                act.activation(squares(n, c), H[:, cut(c), :], ACT.Square).then_inc(ln_sq, 1)

            def deviation(n, c):
                act.wait_ge(ln_var, c + (n * CH + 1))
                act.nop(nofuse=True)
                act.activation(st2[:, cut(c)], st2[:, cut(c)], ACT.Sqrt).then_inc(ln_dev, 1)

            def rectify(n, c):
                act.wait_ge(ln_scl, c + (n * CH + 1))
                act.nop(nofuse=True)
                act.activation(H[:, cut(c), :], H[:, cut(c), :], ACT.Relu).then_inc(tab_ready[n] if n < 2 else h_new, 1)

            def norm_stats(n):
                for c in range(CH):
                    square(n, c)
                act.wait_ge(ln_var, (n + 1) * CH)
                act.activation(st2[:, :], st2[:, :], ACT.Sqrt).then_inc(ln_dev, CH)

            def dense(d):
                def stage(g, i):
                    act.wait_ge(d_tr, g * DU + (d * NB + max(i + 1, 4)))
                    b = g * DU + i
                    if d == 0:
                        act.copy(stg[:, i % 4, 0:D], H[:, bass.DynSlice(b, 1), :].rearrange("p a f -> p (a f)"))
                        act.copy(stg[:, i % 4, D:2 * D], A[:, bass.DynSlice(b, 1), :].rearrange("p a f -> p (a f)")).then_inc(d_st, 1)
                    else:
                        act.copy(stg[:, i % 4, 0:D], H[:, bass.DynSlice(b, 1), :].rearrange("p a f -> p (a f)")).then_inc(d_st, 1)

                def relu(g, i):
                    act.wait_ge(d_m1, g * DU + (d * NB + i + 1))
                    act.activation(rT[0:D, i % 4, :], PS[0:D, 2 + i % 2, 0:P], ACT.Relu, bias=b1c[:, 0:1]).then_inc(d_re, 1)

                def blocks(g, extra):
                    if d in (1, 2):
                        act.wait_ge((h_sum, dv_div)[d - 1], g + 1)
                    if d == 1:
                        lagged(DU, (0, lambda i: stage(g, i)), (3, lambda i: relu(g, i)), extra=extra)
                    else:
                        lagged(DU, (0, lambda i: stage(g, i)), extra=extra)

                n = {0: 1, 2: 3}.get(d)
                chunk_loop(act, blocks, after=() if n is None else (
                    (6, lambda c: square(n, c)), (10, lambda c: deviation(n, c)), (13, lambda c: rectify(n, c))))

            norm_stats(0)
            for c in range(CH):
                rectify(0, c)
            act.wait_ge(added, 1 + STEPS)
            dense(0)

            def relu_message(g, k):
                act.wait_ge(pre_rdy, g * RING + (k + 1))
                act.activation(msg[:, k % 4, 0:D], pre[:, k % 4, 0:D], ACT.Relu).then_inc(msg_rdy, 1)

            tregs = [act.alloc_register(f"tile{k}") for k in range(RING)]

            def load_edge_features(g, k):
                if k % HALF == 0:
                    act.load(tregs[k:k + HALF], trow[0:1, bass.DynSlice(g * RING + k, HALF)])
                t = act.snap(tregs[k], min_val=0, max_val=TR - 1)
                act.dma_start(eatt[0:DE, k, :], eaT[bass.DynSlice(t, 1), :, :].rearrange("a f e -> (a f) e")).then_inc(eah[k], 16)

            for k in range(RING):
                load_edge_features(0, k)
            pipelined(act, (0, relu_message), (-RING, load_edge_features))
            dense(1)
            for c in range(CH):
                act.wait_ge(bn_cen, c + 1)
                act.activation(A[:, cut(c), :], H[:, cut(c), :], ACT.Square).then_inc(bn_sq, 1)
            act.wait_ge(s_v2a, 1)
            act.activation(bs[:, 1, :], bs[:, 1, :], ACT.Sqrt).then_inc(s_a2v, 1)
            for c in range(CH):
                act.wait_ge(bn_aff, c + 1)
                act.activation(H[:, cut(c), :], H[:, cut(c), :], ACT.Relu).then_inc(bn_rel, 1)
            norm_stats(2)
            for c in range(CH):
                act.wait_ge(ln_scl, 2 * CH + c + 1)
                link(act.activation(H[:, cut(c), :], H[:, cut(c), :], ACT.Relu))
                act.activation(A2[:, cut(c), 0:D], H[:, cut(c), :], ACT.Exp, bias=col[:, 3:4]).then_inc(h_new, 1)
            dense(2)
            act.wait_ge(h_new, 2 * CH)
            dense(3)

            act.wait_ge(s_v2a, 2)

            def off_block(g, k):
                act.wait_ge(gat[k], gat_val(3, g))
                act.activation(zb[:, k % 8, :], iota[:, :], ACT.Abs, bias=dstl[:, bass.DynSlice(g * RING + k, 1)],
                               scale=BIG).then_inc(z_rdy, 1)

            def weights(g, k):
                act.wait_ge(xrd, g * RING + (k + 1))
                act.activation(sel[:, k % 4 - 1:k % 4 + 1, :], logit[:, k % 8 - 1:k % 8 + 1, :], ACT.Exp, scale=-1.0).then_inc(prd, 2)

            def rescale(g, k):
                act.wait_ge(lcn, g * RING + (k + 2))
                act.activation(fac[:, k:k + 1], old[:, k:k + 1], ACT.Exp, bias=ln_[:, k:k + 1], scale=-1.0)

            pipelined(act, (0, off_block), (6, rescale), (8, weights, "pair"))
            for c in range(CH):
                act.wait_ge(out_in, c + 1)
                act.activation(H[:, cut(c), :], H[:, cut(c), :], ACT.Tanh).then_inc(out_tanh, 1)

        @block.vector
        def _(dve):
            n = [0]

            def link(ins):
                n[0] += 1
                ins.then_inc(s_dch, 1)
                dve.wait_ge(s_dch, n[0])

            dve.wait_ge(s_in, 16)
            dve.tensor_copy(bcast_src[0:1, 0:TR], cmp[0:1, 0:TR].bitcast(I32)).then_inc(s_dp, 1)
            dve.wait_ge(s_io, 10)
            dve.wait_ge(s_pp, 1)
            q = TR // 4
            for i in range(4):
                ins = dve.tensor_scalar(cmp[:, i * q:(i + 1) * q], PS[:, i, 0:q], col[:, 1:2], None, ALU.is_lt)
            link(ins)
            link(dve.reduce_sum(col[:, 2:3], cmp[:, 0:TR], axis=AX))
            link(dve.tensor_tensor(col[:, 2:3], col[:, 2:3], col[:, 0:1], ALU.add))
            dve.tensor_scalar(reach, reach, col[:, 2:3], None, ALU.is_gt).then_inc(s_dp, 1)
            dve.wait_ge(s_pp, 2)
            link(dve.tensor_copy(bcol[:, :], PS[:, 4, 0:SCH]))
            q = SW // 4
            for i in range(4):
                ins = dve.tensor_copy(brow[:, i * q:(i + 1) * q], PS[0:1, (5, 6, 7, 0)[i], 0:q])
            link(ins)
            link(dve.tensor_tensor(tcol[:, :], scol[:, :], bcol[:, :], ALU.subtract))
            dve.tensor_copy(ti[:, :], tcol[:, :]).then_inc(s_dp, 1)
            dve.wait_ge(s_io, 10)
            for i in range(4):
                link(dve.tensor_scalar(bcast_src[0:1, i * q:(i + 1) * q], PS[0:1, (5, 6, 7, 0)[i], 0:q], -1.0, None, ALU.mult))
            link(dve.tensor_tensor(bcast_src[0:1, 0:SW], bcast_src[0:1, 0:SW], srow[0:1, 0:SW], ALU.add))
            link(dve.tensor_copy(trow[:, :], bcast_src[0:1, 0:SW]))
            link(dve.tensor_copy(srow[0:1, 0:SW], brow[:, :]))
            link(dve.tensor_tensor(bcast_src[0:1, 1:SW], srow[0:1, 1:SW], srow[0:1, 0:SW - 1], ALU.not_equal))
            link(dve.tensor_scalar(bcast_src[0:1, 1:SW], bcast_src[0:1, 1:SW], BIG, None, ALU.mult))
            dve.memset(bcast_src[0:1, 0:1], BIG).then_inc(s_nb, 1)
            link(dve.tensor_scalar(bcol[:, :], bcol[:, :], float(P), None, ALU.mult))
            def chunk_of(c):
                return c.unsqueeze(2).broadcast_to([P, DU, D])

            def centre(n, c):
                at = c + (n * CH + 1)
                dve.reduce_sum(st1[:, cut(c)], X[:, cut(c), :], axis=AX).then_inc(ln_sum, 1)
                dve.wait_ge(ln_sum, at)
                dve.tensor_scalar(st1[:, cut(c)], st1[:, cut(c)], 1.0 / D, None, ALU.mult).then_inc(ln_mean, 1)
                dve.wait_ge(ln_mean, at)
                dve.tensor_tensor(H[:, cut(c), :], X[:, cut(c), :], chunk_of(st1[:, cut(c)]), ALU.subtract).then_inc(ln_cen, 1)

            def variance(n, c):
                at = c + (n * CH + 1)
                dve.wait_ge(ln_sq, at)
                dve.reduce_sum(st2[:, cut(c)], squares(n, c), axis=AX).then_inc(ln_ssq, 1)
                dve.wait_ge(ln_ssq, at)
                dve.tensor_scalar(st2[:, cut(c)], st2[:, cut(c)], 1.0 / D, LN_EPS, ALU.mult, ALU.add).then_inc(ln_var, 1)

            def inverse(n, c):
                dve.wait_ge(ln_dev, c + (n * CH + 1))
                dve.nop(nofuse=True)
                dve.reciprocal(st2[:, cut(c)], st2[:, cut(c)]).then_inc(ln_inv, 1)

            def scale(n, c):
                dve.wait_ge(ln_inv, c + (n * CH + 1))
                dve.tensor_tensor(H[:, cut(c), :], H[:, cut(c), :], chunk_of(st2[:, cut(c)]), ALU.mult).then_inc(ln_scl, 1)

            def norm_stats(n):
                lagged(CH, (0, lambda c: centre(n, c)), (1, lambda c: variance(n, c)))
                dve.wait_ge(ln_dev, (n + 1) * CH)
                dve.reciprocal(st2[:, :], st2[:, :]).then_inc(ln_inv, CH)

            dve.wait_ge(s_w, 16 * 18)
            norm_stats(0)
            for c in range(CH):
                scale(0, c)
            dve.wait_ge(s_er, 16 * 3 * SCH)
            for c in range(SCH):
                dve.tensor_copy(erow[0][:, c, :], erow[0][:, c, :].bitcast(I32))
                ins = dve.tensor_scalar(erow[1][:, c, :], erow[1][:, c, :].bitcast(I32), bcol[:, c:c + 1], None, ALU.subtract)
            ins.then_inc(s_dp, 1)
            for i in range(3 * SCH):
                dve.wait_ge(s_pp, 2 + i + 1)
                t = (idx, dstl, wst)[i % 3]
                dve.tensor_copy(t[:, i // 3 * P:(i // 3 + 1) * P], PS[:, i % 8, 0:P]).then_inc(s_dp, 1)
            dve.wait_ge(s_w, 16 * 18)
            dve.wait_ge(s_nbd, 16)
            dve.wait_ge(s_pp, 2 + 3 * SCH + 1)
            dve.memset(w4x[0:D, D:D + 1], 0.0)
            link(dve.memset(w4x[D:D + 1, :], 0.0))
            dve.memset(w4x[D:D + 1, D:D + 1], 1.0)
            dve.tensor_copy(w4x[0:D, D + 1:D + 3], PS[0:D, 0, 0:2])
            dve.memset(col[:, 3:4], SOFT_EPS)
            link(dve.tensor_scalar(col[:, 4:5], col[:, 0:1], float(z.LAST), None, ALU.is_lt))

            def invert(b, count):
                e = A2[:, bass.DynSlice(b, count), 0:D]
                dve.reciprocal(e, e).then_inc(dv_inv, count)

            def dense(d):
                def turned_copy(g, i):
                    dve.wait_ge(d_tr, g * DU + (d * NB + i + 5))
                    w = 2 * P if d == 0 else P
                    dve.tensor_copy(tT[0:D, i % 4, 0:w], PS[0:D, i % 2, 0:w]).then_inc(d_tc, 1)

                    if d == 2 and i < DU // 2 and not (isinstance(g, int) and g == CH - 1):
                        invert(g * DU + (2 * i + DU), 2)

                def finish(g, i):
                    b = g * DU + i
                    if d == 1:
                        dve.wait_ge(d_m2, g * DU + (i + 1))
                        dve.tensor_copy(H[:, bass.DynSlice(b, 1), :].rearrange("p a f -> p (a f)"), PS[:, 4 + i % 4, 0:D]).then_inc(d_po, 1)
                        return
                    dve.wait_ge(d_m1, g * DU + (d * NB + i + 1))
                    if d == 3:
                        dve.tensor_copy(A3[:, bass.DynSlice(b, 1), :].rearrange("p a f -> p (a f)"), PS[:, 2 + i % 4, 0:D + 2])
                        dve.tensor_copy(adc[:, bass.DynSlice(b, 1)], PS[:, 2 + i % 4, D + 2:D + 3]).then_inc(d_po, 1)
                    else:
                        xb = X[:, bass.DynSlice(b, 1), :].rearrange("p a f -> p (a f)")
                        dve.tensor_tensor(xb, xb, PS[:, 2 + i % 4, 0:D], ALU.add).then_inc(d_po, 1)

                def blocks(g, extra):
                    lagged(DU, (0, lambda i: turned_copy(g, i)), (3 if d == 1 else 2, lambda i: finish(g, i)), extra=extra)

                def centre_after(n, c):
                    dve.wait_ge(d_po, c * DU + (d * NB + DU))
                    centre(n, c)

                if d < 3:
                    link(dve.memset(ones_rows, 1.0))
                n = {0: 1, 2: 3}.get(d)
                if d == 2:
                    invert(0, DU)
                chunk_loop(dve, blocks, after=() if n is None else (
                    (2, lambda c: centre_after(n, c)), (5, lambda c: variance(n, c)), (8, lambda c: inverse(n, c)),
                    (9, lambda c: scale(n, c))))
                dve.wait_ge(d_po, (d + 1) * NB)

            regs = [dve.alloc_register(f"dve_block{k}") for k in range(RING)]

            def load_blocks(g, k):
                dve.load(regs[k:k + HALF], brow[0:1, bass.DynSlice(g * RING + k, HALF)])

            def steps(L):
                base, add_base = L * STEPS, L * (STEPS + 1) + 1
                acc, W = ((A, D), (A, D), (A2, 2 * D))[L]

                def one_hot(g, k):
                    s = g * RING + k
                    if L == 0:
                        dve.tensor_scalar(sel[:, k % 4, :], iota[:, :], dstl[:, bass.DynSlice(s, 1)], wst[:, bass.DynSlice(s, 1)],
                                          ALU.is_equal, ALU.mult).then_inc(sel_rdy, 1)
                    else:
                        dve.tensor_scalar(sel[:, k % 4, :], iota[:, :], dstl[:, bass.DynSlice(s, 1)], None,
                                          ALU.is_equal).then_inc(sel_rdy, 1)

                def pre_message(g, k):
                    dve.wait_ge(ea_mm, g * RING + (k + 1))
                    dve.wait_ge(gat[k], gat_val(L, g))
                    dve.tensor_tensor(pre[:, k % 4, 0:D], ering[:, k, 0:D], PS[:, 4 + k % 4, 0:D], ALU.add).then_inc(pre_rdy, 1)

                def add(g, k):
                    b = dve.snap(regs[k], min_val=0, max_val=NB - 1)
                    ab = acc[:, bass.DynSlice(b, 1), :].rearrange("p a f -> p (a f)")
                    dve.wait_ge(slot_free, g * RING + (base + RING + k + 1))
                    dve.wait_ge(added, g * RING + (add_base + k))
                    dve.tensor_tensor(ab, ab, PS[:, k % 4, 0:W], ALU.add).then_inc(added, 1)

                if L == 2:
                    dve.memset(acc[:, :, 0:D], NO_EDGE)
                    dve.memset(acc[:, :, D:2 * D], 0.0).then_inc(added, 1)
                else:
                    dve.memset(acc, 0.0).then_inc(added, 1)
                if L == 1:
                    pipelined(dve, (0, one_hot), (0, pre_message), (3, add), load=load_blocks)
                else:
                    pipelined(dve, (0, one_hot), (2, add), load=load_blocks)
                dve.wait_ge(added, add_base + STEPS)

            dve.memset(eatt[DE:DE + 1, :, :], 1.0).then_inc(ea_ones, 1)
            steps(0)
            dense(0)
            steps(1)
            dense(1)
            link(dve.tensor_scalar(H[:, NB - 1, :], H[:, NB - 1, :], col[:, 4:5], None, ALU.mult))
            dve.reduce_sum(bs[:, 0, :], H.rearrange("p b f -> p f b"), axis=AX).then_inc(s_bnp, 1)
            dve.wait_ge(s_bnp, 2)
            link(dve.tensor_scalar(bs[:, 2, :], PS[:, 0, 0:D], 1.0 / z.N, None, ALU.mult))

            def row_of(r):
                return r.unsqueeze(1).broadcast_to([P, DU, D])

            def bn_centre(c):
                ins = dve.tensor_tensor(H[:, cut(c), :], H[:, cut(c), :], row_of(bs[:, 2, :]), ALU.subtract)
                if c == CH - 1:
                    link(ins)
                    ins = dve.tensor_scalar(H[:, NB - 1, :], H[:, NB - 1, :], col[:, 4:5], None, ALU.mult)
                ins.then_inc(bn_cen, 1)

            for c in range(CH):
                bn_centre(c)
            dve.wait_ge(bn_sq, CH)
            dve.reduce_sum(bs[:, 1, :], A.rearrange("p b f -> p f b"), axis=AX).then_inc(s_bnp, 1)
            dve.wait_ge(s_bnp, 4)
            dve.tensor_scalar(bs[:, 1, :], PS[:, 1, 0:D], 1.0 / z.N, BN_EPS, ALU.mult, ALU.add).then_inc(s_v2a, 1)
            dve.wait_ge(s_a2v, 1)
            link(dve.reciprocal(bs[:, 1, :], bs[:, 1, :]))
            link(dve.tensor_tensor(bs[:, 1, :], bs[:, 1, :], bn[:, 0, :], ALU.mult))

            def bn_affine(c):
                link(dve.tensor_tensor(H[:, cut(c), :], H[:, cut(c), :], row_of(bs[:, 1, :]), ALU.mult))
                dve.tensor_tensor(H[:, cut(c), :], H[:, cut(c), :], row_of(bn[:, 1, :]), ALU.add).then_inc(bn_aff, 1)

            def bn_residual(c):
                dve.wait_ge(bn_rel, c + 1)
                link(dve.tensor_tensor(X[:, cut(c), :], X[:, cut(c), :], H[:, cut(c), :], ALU.add))

            lagged(CH, (0, bn_affine), (1, bn_residual))
            norm_stats(2)

            def exp_times(c):
                dve.wait_ge(h_new, c + 1)
                dve.scalar_tensor_tensor(out=A2[:, cut(c), D:2 * D], in0=H[:, cut(c), :], scalar=SOFT_EPS, in1=A2[:, cut(c), 0:D],
                                         op0=ALU.add, op1=ALU.mult).then_inc(tab_ready[2], 1)

            lagged(CH, (0, lambda c: scale(2, c)), (2, exp_times))
            dve.wait_ge(tab_wr[2], 16 * CH)
            steps(2)
            dense(2)
            dve.wait_ge(h_new, 2 * CH)
            dense(3)
            dve.sem_inc(added, 1)
            add_base = 3 * (STEPS + 1) + 1
            dve.wait_ge(s_adT, 1)
            dve.tensor_copy(adT[:, :], PS[0:NB, 6, 0:P]).then_inc(s_adS, 1)
            dve.wait_ge(added, add_base)
            link(dve.tensor_tensor(lc[:, :], A3[:, :, D + 1:D + 2].rearrange("p b a -> p (b a)"), adc[:, :], ALU.add))
            link(dve.scalar_tensor_tensor(out=lc[:, :], in0=lc[:, :], scalar=SLOPE, in1=lc[:, :], op0=ALU.mult, op1=ALU.max))
            link(dve.tensor_scalar(lc[:, :], lc[:, :], -1.0, None, ALU.mult))
            dve.tensor_scalar(dstl[:, :], dstl[:, :], -BIG, None, ALU.mult).then_inc(s_v2a, 1)
            dve.wait_ge(tab_wr[3], 16 * CH)
            dve.wait_ge(s_adR, 16)

            base = 3 * STEPS

            late = [dve.alloc_register(f"dve_late_block{k}") for k in range(2)]

            def next_blocks(g, k):
                if k % HALF == 0:
                    if not (isinstance(g, int) and g == 0):
                        for j in range(2):
                            dve.reg_mov(late[j], regs[k + HALF - 2 + j])
                    load_blocks(g, k)

            def raw_logits(g, k):
                b = dve.snap(regs[k], min_val=0, max_val=NB - 1)
                dve.wait_ge(z_rdy, g * RING + (k + 1))
                dve.scalar_tensor_tensor(out=raw[:, k % 4, :], in0=zb[:, k % 8, :], scalar=ering[:, k, D + 1:D + 2],
                                         in1=adrow[:, bass.DynSlice(b * P, P)], op0=ALU.subtract, op1=ALU.subtract)\
                    .then_inc(raw_rdy, 1)

            def leaky(g, k):
                dve.wait_ge(raw_rdy, g * RING + (k + 1))
                dve.wait_ge(prd, g * RING + (k + 1))
                z = raw[:, k % 4 - 1:k % 4 + 1, :]
                dve.scalar_tensor_tensor(out=logit[:, k % 8 - 1:k % 8 + 1, :], in0=z, scalar=SLOPE, in1=z,
                                         op0=ALU.mult, op1=ALU.min).then_inc(u_rdy, 2)

            def tile_max(g, k):
                dve.wait_ge(psa, g * RING + (k + 1))
                dve.tensor_reduce(cm[:, k - 1:k + 1], PS[:, k // 2 % 2, 0:2 * P].rearrange("p (s e) -> p s e", s=2), AX, ALU.min)\
                    .then_inc(cmx, 2)

            def old_max(g, k):
                b = dve.snap(regs[k], min_val=0, max_val=NB - 1)
                before = ln_[:, (k - 1) % RING:(k - 1) % RING + 1]
                dve.wait_ge(lcn, g * RING + (k + 1))
                dve.scalar_tensor_tensor(out=old[:, k:k + 1], in0=before, scalar=wst[:, bass.DynSlice(g * RING + k, 1)],
                                         in1=lc[:, bass.DynSlice(b, 1)], op0=ALU.add, op1=ALU.min).then_inc(oldr, 1)

            def new_max(g, k):
                dve.wait_ge(oldr if k % 2 else cmx, g * RING + (k + 1))
                dve.tensor_tensor(ln_[:, k:k + 1], cm[:, k:k + 1], old[:, k:k + 1], ALU.min).then_inc(lcn, 1)

            def shifted(g, k):
                dve.wait_ge(psc, g * RING + (k + 1))
                z = logit[:, k % 8 - 1:k % 8 + 1, :]
                dve.tensor_tensor(z, z, PS[:, 2 + k // 2 % 2, 0:2 * P].rearrange("p (s e) -> p s e", s=2), ALU.subtract)\
                    .then_inc(xrd, 2)

            def add_scaled(g, k):
                moved = k % HALF >= HALF - 2 and not (isinstance(g, int) and g == ITERS - 1)
                b = dve.snap(late[k % 2] if moved else regs[k], min_val=0, max_val=NB - 1)
                ab = A3[:, bass.DynSlice(b, 1), 0:D + 1].rearrange("p a f -> p (a f)")
                if isinstance(g, int):
                    dve.wait_ge(added, g * RING + (add_base + k))
                dve.wait_ge(slot_free, g * RING + (base + RING + k + 1))
                dve.scalar_tensor_tensor(out=ab, in0=ab, scalar=fac[:, k:k + 1], in1=PS[:, 4 + k % 4, 0:D + 1],
                                         op0=ALU.mult, op1=ALU.add).then_inc(added, 1)

            dve.memset(ln_[:, RING - 1:RING], 0.0).then_inc(lcn, 1)
            dve.wait_ge(s_nbl, 16)
            pipelined(dve, (12, add_scaled), (8, shifted, "pair"), (1, next_blocks), (6, old_max), (5, tile_max, "pair"), (2, raw_logits),
                      (3, leaky, "pair"), (6, new_max))
            dve.wait_ge(added, add_base + STEPS)
            den = A3[:, :, D:D + 1].rearrange("p b a -> p (b a)")
            link(dve.tensor_scalar(st1[:, :], den, GAT_EPS, None, ALU.add))
            link(dve.reciprocal(st1[:, :], st1[:, :]))

            def attended(c):
                link(dve.tensor_tensor(H[:, cut(c), :], A3[:, cut(c), 0:D], chunk_of(st1[:, cut(c)]), ALU.mult))
                dve.tensor_tensor(H[:, cut(c), :], H[:, cut(c), :], row_of(bn[:, 2, :]), ALU.add).then_inc(out_in, 1)

            def result(c):
                dve.wait_ge(out_tanh, c + 1)
                dve.tensor_tensor(X[:, cut(c), :], X[:, cut(c), :], H[:, cut(c), :], ALU.add).then_inc(s_fin, 1)

            lagged(CH, (0, attended), (1, result))


def kernel(x, src, dst, edge_attr_32, edge_weight, L0_gnn_mlp_w, L0_gnn_mlp_b, L1_gnn_We, L1_gnn_be, L1_gnn_W1,
           L1_gnn_b1, L1_gnn_W2, L1_gnn_b2, L1_gnn_gamma, L1_gnn_beta, L2_gnn_W, L2_gnn_b, L3_gnn_W,
           L3_gnn_att_src, L3_gnn_att_dst, L3_gnn_bias):
    import concourse.bacc as bacc
    from concourse.bass_utils import run_bass_kernel_spmd as run

    z = Sizes(x.shape[0], src.shape[0])

    def rows(a, fill):
        a = np.asarray(a)
        full = np.full((z.TR * P,) + a.shape[1:], fill, a.dtype)
        full[:a.shape[0]] = a
        return full.reshape((z.TR, P) + a.shape[1:])

    arrays = {
        "x": np.asarray(x), "src": rows(src, 0), "dst": rows(dst, NO_NODE), "ew": rows(edge_weight, 0),
        "eaT": rows(edge_attr_32, 0).transpose(0, 2, 1),
        "w0T": np.asarray(L0_gnn_mlp_w).T, "b0": L0_gnn_mlp_b, "We": L1_gnn_We, "be": L1_gnn_be, "W1": L1_gnn_W1,
        "b1": L1_gnn_b1, "W2": L1_gnn_W2, "b2": L1_gnn_b2, "gamma": L1_gnn_gamma, "beta": L1_gnn_beta,
        "W3": L2_gnn_W, "b3": L2_gnn_b, "W4": L3_gnn_W, "W4T": np.asarray(L3_gnn_W).T,
        "att": np.stack([np.asarray(L3_gnn_att_src), np.asarray(L3_gnn_att_dst)], axis=1), "bias4": L3_gnn_bias,
    }
    arrays = {k: np.ascontiguousarray(a) for k, a in arrays.items()}
    nc = bacc.Bacc("TRN2", target_bir_lowering=False, num_devices=1)
    aps = {k: nc.dram_tensor(f"in_{k}", a.shape, mybir.dt.from_np(a.dtype), kind="ExternalInput").ap()
           for k, a in arrays.items()}
    out = nc.dram_tensor("out_0", tuple(x.shape), F32, kind="ExternalOutput").ap()
    build(nc, z, out=out, **aps)
    r = run(nc, [{f"in_{k}": a for k, a in arrays.items()}], core_ids=[0])
    return r.results[0]["out_0"]
```
